# Optimizing a Trainium2 kernel written in Bass

```python
import numpy as np
import jax
import jax.numpy as jnp

def _softmax(x, axis=-1):
    return jax.nn.softmax(x, axis=axis)

def _gelu(x):
    return jax.nn.gelu(x, approximate=True)

def _silu(x):
    return jax.nn.silu(x)

def _sigmoid(x):
    return jax.nn.sigmoid(x)

def _layernorm(x, axis=-1, eps=1e-05):
    m = jnp.mean(x, axis=axis, keepdims=True)
    v = jnp.var(x, axis=axis, keepdims=True)
    return (x - m) / jnp.sqrt(v + eps)

def _scatter_add(tgt, idx, src, axis=0):
    return tgt.at[idx].add(src)

def _segment_sum(src, seg, n):
    return jax.ops.segment_sum(src, seg, n)
kernel_name = 'mk_xattn_seq_d2_seqx_r2_f21963'

def setup_inputs(seed: int=0):
    np.random.seed(seed)
    _w = jnp.asarray

    def _rec_inputs():
        import jax
        import jax.numpy as jnp
        _rk = jax.random.key(seed)
        x = 7.22e-05 + 1 * jax.random.normal(jax.random.fold_in(_rk, 1), (4, 1024, 512), jnp.float32)
        _lenS = 1024 - jax.random.randint(jax.random.fold_in(_rk, 7), (4,), 0, max(1, 1024 // 4) + 1, jnp.int32)
        _lenS2 = 1024 - jax.random.randint(jax.random.fold_in(_rk, 8), (4,), 0, max(1, 1024 // 4) + 1, jnp.int32)
        _ctx_1024P = jax.random.normal(jax.random.fold_in(_rk, 11), (4, 16, 512), jnp.float32)
        _ctx_1024c = jax.random.dirichlet(jax.random.fold_in(_rk, 511), 0.3 * jnp.ones((16,), jnp.float32), (4, 1024))
        _ctx_1024t = jnp.einsum('bsk,bkd->bsd', _ctx_1024c, _ctx_1024P)
        _ctx_1024t = _ctx_1024t * jax.lax.rsqrt(jnp.mean(jnp.square(_ctx_1024t)) + 1e-12) * 0.953939
        ctx_1024 = 4.13588e-05 + 0.999923 * (_ctx_1024t + 0.3 * jax.random.normal(jax.random.fold_in(_rk, 611), (4, 1024, 512), jnp.float32))
        return (x, ctx_1024)
    x, ctx_1024 = _rec_inputs()

    def _L0_xattn_setup():
        import jax, jax.numpy as jnp
        import numpy as np
        D_MODEL = 512
        N_HEAD = 16
        D_K = D_MODEL // N_HEAD
        LN_EPS = 1e-05

        def _mha(q, k, v, Wq, bq, Wk, bk, Wv, bv, Wo, bo, gamma, beta):
            B, S, _ = q.shape
            Q = (q @ Wq.T + bq).reshape(B, S, N_HEAD, D_K).transpose(0, 2, 1, 3)
            K = (k @ Wk.T + bk).reshape(B, S, N_HEAD, D_K).transpose(0, 2, 1, 3)
            V = (v @ Wv.T + bv).reshape(B, S, N_HEAD, D_K).transpose(0, 2, 1, 3)
            score = jnp.einsum('bhqd,bhkd->bhqk', Q, K) / jnp.sqrt(jnp.float32(D_K))
            att = jax.nn.softmax(score, axis=-1)
            out = jnp.einsum('bhqk,bhkd->bhqd', att, V)
            out = out.transpose(0, 2, 1, 3).reshape(B, S, D_MODEL)
            out = out @ Wo.T + bo
            x = out + q
            mu = jnp.mean(x, axis=-1, keepdims=True)
            var = jnp.mean((x - mu) ** 2, axis=-1, keepdims=True)
            return (x - mu) * jax.lax.rsqrt(var + LN_EPS) * gamma + beta
        key = jax.random.key(seed)
        ks = jax.random.split(key, 12)
        B, S = (4, 1024)
        s = 1.0 / np.sqrt(D_MODEL)
        return {'q': jax.random.normal(ks[0], (B, S, D_MODEL), jnp.float32), 'k': jax.random.normal(ks[1], (B, S, D_MODEL), jnp.float32), 'v': jax.random.normal(ks[2], (B, S, D_MODEL), jnp.float32), 'Wq': jax.random.normal(ks[3], (D_MODEL, D_MODEL), jnp.float32) * s, 'bq': jnp.zeros((D_MODEL,), jnp.float32), 'Wk': jax.random.normal(ks[4], (D_MODEL, D_MODEL), jnp.float32) * s, 'bk': jnp.zeros((D_MODEL,), jnp.float32), 'Wv': jax.random.normal(ks[5], (D_MODEL, D_MODEL), jnp.float32) * s, 'bv': jnp.zeros((D_MODEL,), jnp.float32), 'Wo': jax.random.normal(ks[6], (D_MODEL, D_MODEL), jnp.float32) * s, 'bo': jnp.zeros((D_MODEL,), jnp.float32), 'gamma': jnp.ones((D_MODEL,), jnp.float32), 'beta': jnp.zeros((D_MODEL,), jnp.float32)}
    _L0_xattn_all = _L0_xattn_setup()
    _L0_xattn_in = {k: v for k, v in _L0_xattn_all.items() if k in ('Wq', 'bq', 'Wk', 'bk', 'Wv', 'bv', 'Wo', 'bo', 'gamma', 'beta')}
    del _L0_xattn_all

    def _L1_xattn_setup():
        import jax, jax.numpy as jnp
        import numpy as np
        LN_EPS = 1e-05
        ATTN_EPS = 1e-06
        key = jax.random.key(seed)
        k1, k2, k3 = jax.random.split(key, 3)
        B, Nq, Nk, D = (8, 1024, 1024, 512)
        return {'query': jax.random.normal(k1, (B, Nq, D), dtype=jnp.float32), 'key': jax.random.normal(k2, (B, Nk, D), dtype=jnp.float32), 'value': jax.random.normal(k3, (B, Nk, D), dtype=jnp.float32), 'gamma': jnp.ones((D,), dtype=jnp.float32), 'beta': jnp.zeros((D,), dtype=jnp.float32)}
    _L1_xattn_all = _L1_xattn_setup()
    _L1_xattn_in = {k: v for k, v in _L1_xattn_all.items() if k in ('gamma', 'beta')}
    del _L1_xattn_all
    return {'x': x, 'ctx_1024': ctx_1024, 'L0_xattn_Wq': _L0_xattn_in['Wq'], 'L0_xattn_bq': _L0_xattn_in['bq'], 'L0_xattn_Wk': _L0_xattn_in['Wk'], 'L0_xattn_bk': _L0_xattn_in['bk'], 'L0_xattn_Wv': _L0_xattn_in['Wv'], 'L0_xattn_bv': _L0_xattn_in['bv'], 'L0_xattn_Wo': _L0_xattn_in['Wo'], 'L0_xattn_bo': _L0_xattn_in['bo'], 'L0_xattn_gamma': _L0_xattn_in['gamma'], 'L0_xattn_beta': _L0_xattn_in['beta'], 'L1_xattn_gamma': _L1_xattn_in['gamma'], 'L1_xattn_beta': _L1_xattn_in['beta']}

def reference(x, ctx_1024, L0_xattn_Wq, L0_xattn_bq, L0_xattn_Wk, L0_xattn_bk, L0_xattn_Wv, L0_xattn_bv, L0_xattn_Wo, L0_xattn_bo, L0_xattn_gamma, L0_xattn_beta, L1_xattn_gamma, L1_xattn_beta):
    import jax
    import jax.numpy as jnp

    def _L0_xattn_ref(q, k, v, Wq, bq, Wk, bk, Wv, bv, Wo, bo, gamma, beta):
        import jax, jax.numpy as jnp
        import numpy as np
        D_MODEL = 512
        N_HEAD = 16
        D_K = D_MODEL // N_HEAD
        LN_EPS = 1e-05

        def _mha(q, k, v, Wq, bq, Wk, bk, Wv, bv, Wo, bo, gamma, beta):
            B, S, _ = q.shape
            Q = (q @ Wq.T + bq).reshape(B, S, N_HEAD, D_K).transpose(0, 2, 1, 3)
            K = (k @ Wk.T + bk).reshape(B, S, N_HEAD, D_K).transpose(0, 2, 1, 3)
            V = (v @ Wv.T + bv).reshape(B, S, N_HEAD, D_K).transpose(0, 2, 1, 3)
            score = jnp.einsum('bhqd,bhkd->bhqk', Q, K) / jnp.sqrt(jnp.float32(D_K))
            att = jax.nn.softmax(score, axis=-1)
            out = jnp.einsum('bhqk,bhkd->bhqd', att, V)
            out = out.transpose(0, 2, 1, 3).reshape(B, S, D_MODEL)
            out = out @ Wo.T + bo
            x = out + q
            mu = jnp.mean(x, axis=-1, keepdims=True)
            var = jnp.mean((x - mu) ** 2, axis=-1, keepdims=True)
            return (x - mu) * jax.lax.rsqrt(var + LN_EPS) * gamma + beta
        return _mha(q, k, v, Wq, bq, Wk, bk, Wv, bv, Wo, bo, gamma, beta)

    def _L1_xattn_ref(query, key, value, gamma, beta):
        import jax, jax.numpy as jnp
        import numpy as np
        LN_EPS = 1e-05
        ATTN_EPS = 1e-06
        Q_phi = jax.nn.elu(query)
        K_phi = jax.nn.elu(key)
        KV = jnp.einsum('bnd,bne->bde', K_phi, value)
        Z = 1.0 / (jnp.einsum('bnd,bd->bn', Q_phi, K_phi.sum(axis=1)) + ATTN_EPS)
        attn = jnp.einsum('bnd,bde->bne', Q_phi, KV) * Z[..., None]
        x = query + attn
        mean = jnp.mean(x, axis=-1, keepdims=True)
        var = jnp.mean(jnp.square(x - mean), axis=-1, keepdims=True)
        return (x - mean) * jax.lax.rsqrt(var + LN_EPS) * gamma + beta
    x = _L0_xattn_ref(x, ctx_1024, ctx_1024, L0_xattn_Wq, L0_xattn_bq, L0_xattn_Wk, L0_xattn_bk, L0_xattn_Wv, L0_xattn_bv, L0_xattn_Wo, L0_xattn_bo, L0_xattn_gamma, L0_xattn_beta)
    x = _L1_xattn_ref(x, ctx_1024, ctx_1024, L1_xattn_gamma, L1_xattn_beta)
    return x

_drawn_inputs = setup_inputs


def setup_inputs(seed=0):
    import zlib

    import numpy as np

    out = dict(_drawn_inputs(seed))
    spreads = {'L0_xattn_bq': (0.0, 0.1),
     'L0_xattn_bk': (0.0, 0.1),
     'L0_xattn_bv': (0.0, 0.1),
     'L0_xattn_bo': (0.0, 0.1),
     'L0_xattn_gamma': (1.0, 0.2),
     'L0_xattn_beta': (0.0, 0.1),
     'L1_xattn_gamma': (1.0, 0.2),
     'L1_xattn_beta': (0.0, 0.1)}
    factors = {}
    for name, (base, spread) in spreads.items():
        noise = np.random.default_rng([zlib.crc32(name.encode()), seed]).standard_normal(out[name].shape)
        drawn = base * np.exp(spread * noise) if base else spread * noise
        out[name] = jnp.asarray(drawn.astype(out[name].dtype))
    for name, factor in factors.items():
        out[name] = (out[name] * factor).astype(out[name].dtype)
    return out
```

```python
from contextlib import ExitStack

import concourse.bass as bass
from concourse import mybir

F32 = mybir.dt.float32
F32R = mybir.dt.float32r
ALU = mybir.AluOpType
ACT = mybir.ActivationFunctionType
AX = mybir.AxisListType


class Stream:

    def __init__(self, engine, sem):
        self.engine, self.sem, self.count, self.seen = engine, sem, 0, {}

    def wait(self, *marks):
        for sem, value in marks:
            if self.seen.get(id(sem), 0) < value:
                self.seen[id(sem)] = value
                self.engine.wait_ge(sem, value)

    def do(self, instruction):
        instruction(self.engine)

    def mark(self, instruction):
        self.count += 1
        instruction(self.engine).then_inc(self.sem, 1)
        return self.sem, self.count


class Landing:

    def __init__(self, sem):
        self.sem, self.count = sem, 0

    def dma(self, stream, start):
        self.count += 16
        stream.do(lambda e: start(e).then_inc(self.sem, 16))

    def mark(self):
        return self.sem, self.count


def build(nc, x, xT, ctx, ctxT, WqT, bq, WkT, bk, WvT, bv, WoT, bo, gamma0, beta0, gamma1, beta1, out):
    B, S, D = x.shape
    P = nc.NUM_PARTITIONS
    DK = 32
    QUAD = P // DK
    G = D // P
    CH = 256
    NC = S // CH
    TPC = CH // P
    KT = S // P
    STEPS = KT
    HALF = 512
    SCALE = float(DK) ** -0.5
    LN_EPS, ATTN_EPS = 1e-5, 1e-6
    LEAD = 3
    LAG = 6
    NQ, NP, NSTAGE = 3, 7, 2
    SPLIT = 3 * DK
    ROWS = SPLIT + 2 * QUAD
    UNITS = NC * G

    with ExitStack() as c:
        def sb(name, shape, dt=F32):
            return c.enter_context(nc.sbuf_tensor(name, shape, dt))

        def ps(name, cols):
            return c.enter_context(nc.psum_tensor(name, [P, cols], F32))

        def sem(name):
            return c.enter_context(nc.semaphore(name))

        wq = sb("wq", [P, G, D])
        wo = sb("wo", [P, G, D])
        k_stack = sb("k_stack", [P, G * QUAD, S], F32R)
        q_stack = sb("q_stack", [P, NQ, QUAD, CH], F32R)
        v_sb = sb("v_sb", [P, KT, D])
        p_ring = sb("p_ring", [P, NP, QUAD * CH])
        pair_sum = sb("pair_sum", [P, 2, QUAD * CH])
        quad_sum = sb("quad_sum", [P, QUAD * CH])
        xT_sb = sb("xT_sb", [P, 2, G, CH])
        stage_h = sb("stage_h", [P, NSTAGE, CH], F32R)
        stage_l = sb("stage_l", [P, NSTAGE, CH], F32R)
        outT = sb("outT", [P, 2, G, CH])
        kv_sb = sb("kv_sb", [P, G, D])
        ksum_sb = sb("ksum_sb", [P, D])
        x_nat = sb("x_nat", [P, 2, D])
        y_sb = sb("y_sb", [P, D])
        x1_sb = sb("x1_sb", [P, D])
        e_sb = sb("e_sb", [P, 2, D])
        phi_sb = sb("phi_sb", [P, D])
        phiT_sb = sb("phiT_sb", [P, D])
        rows_sb = {n: sb(n + "_row", [P, D]) for n in ("bv", "bo", "gamma0", "beta0", "gamma1", "beta1")}
        bq_col = sb("bq_col", [P, G])
        bk_col = sb("bk_col", [P, G])
        ident = sb("ident", [P, P])
        ones = sb("ones", [P, P])
        onehot = sb("onehot", [P, QUAD])
        maxes = sb("maxes", [P, 2, 2, TPC, QUAD])
        max_row = sb("max_row", [P, TPC, QUAD])
        neg_max = sb("neg_max", [P, 2, TPC, 2 * QUAD], F32R)
        stats = sb("stats", [P, 6])
        mean_var = sb("mean_var", [P, 2])
        var_eps = sb("var_eps", [P, 1])
        rstd = sb("rstd", [P, 1])
        minus_half = sb("minus_half", [P, 1])
        z_sb = sb("z_sb", [P, 3])
        wk = p_ring[:, 0:2, :].rearrange("p a n -> p (a n)").rearrange("p (t n) -> p t n", t=G)
        wv = p_ring[:, 2:4, :].rearrange("p a n -> p (a n)").rearrange("p (t n) -> p t n", t=G)
        ctxT_sb = [p_ring[:, 4 + i, :].rearrange("p (t n) -> p t n", t=G) for i in range(2)]
        ctx_nat = [p_ring[:, 6, i * D:(i + 1) * D] for i in range(2)]

        scoreT = [ps(f"scoreT{i}", 2 * HALF) for i in range(2)]
        score = [ps(f"score{i}", HALF) for i in range(2)]
        acc = ps("acc", HALF)
        misc = ps("misc", HALF)

        pe, act, dve, pool, sp = (Stream(engine, sem(name)) for engine, name in (
            (nc.tensor, "pe"), (nc.scalar, "act"), (nc.vector, "dve"), (nc.gpsimd, "pool"), (nc.sync, "sp")))
        land = {n: Landing(sem("dma_" + n)) for n in
                ("wq", "wo", "wk", "wv", "rows", "cols", "xT0", "xT1", "ctxT0", "ctxT1",
                 "ctx_nat0", "ctx_nat1", "x_nat0", "x_nat1", "out0", "out1")}
        free = {}

        def released(name):
            return free.get(name, [])

        for name, src in (("bv", bv), ("bo", bo), ("gamma0", gamma0), ("beta0", beta0),
                          ("gamma1", gamma1), ("beta1", beta1)):
            land["rows"].dma(sp, lambda e, n=name, s=src: e.dma_start(
                rows_sb[n][:], s.partition_broadcast(P)))
        for dst, src in ((bq_col, bq), (bk_col, bk)):
            land["cols"].dma(sp, lambda e, d=dst, s=src: e.dma_start(
                d[:], s.rearrange("(t p) -> p t", p=P), allow_slow_non_contiguous=True))
        land["wq"].dma(sp, lambda e: e.dma_start(wq[:], WqT.rearrange("(t p) n -> p t n", p=P)))
        land["wo"].dma(sp, lambda e: e.dma_start(wo[:], WoT.rearrange("(t p) n -> p t n", p=P)))

        cleared = pool.mark(lambda e: e.memset(ident[:], 0.0))
        hot_cleared = pool.mark(lambda e: e.memset(onehot[:], 0.0))
        pool.wait(cleared)
        ident_ready = pool.mark(lambda e: e.affine_select(
            out=ident[:], in_=ident[:], compare_op=ALU.not_equal, fill=1.0, base=0,
            pattern=[[-1, P]], channel_multiplier=1))
        hot = hot_cleared
        for r in range(2):
            pool.wait(hot)
            hot = pool.mark(lambda e, r=r: e.affine_select(
                out=onehot[:], in_=onehot[:], compare_op=ALU.not_equal, fill=1.0,
                base=-(SPLIT + r * QUAD), pattern=[[-1, QUAD]], channel_multiplier=1))
        ones_ready = pool.mark(lambda e: e.memset(ones[:], 1.0))
        half_ready = pool.mark(lambda e: e.memset(minus_half[:], -0.5))
        dve.wait(hot)
        for g in range(G):
            hot_ready = dve.mark(lambda e, g=g: e.tensor_copy(
                k_stack[SPLIT:ROWS, g * QUAD:(g + 1) * QUAD, :],
                onehot[SPLIT:ROWS, :].unsqueeze(2).to_broadcast([2 * QUAD, QUAD, S])))

        n_stage = [0]
        stage_land = [Landing(sem(f"dma_stage{i}")) for i in range(NSTAGE)]

        def project_split(weight, bias, src, g, bank, bank_name, bias_ready):
            slot = n_stage[0] % NSTAGE
            n_stage[0] += 1
            pe.wait(*released(bank_name))
            for t in range(G):
                step = lambda e, t=t: e.matmul(bank, weight[:, t, g * P:(g + 1) * P], src[:, t, :],
                                               start=t == 0, stop=t == G - 1)
                pe.do(step) if t < G - 1 else None
            projected = pe.mark(step)
            act.wait(projected, bias_ready, stage_land[slot].mark())
            high = act.mark(lambda e: e.activation(stage_h[:, slot, :], bank, ACT.Identity,
                                                   bias=bias[:, g:g + 1]))
            dve.wait(projected, high, stage_land[slot].mark())
            low = dve.mark(lambda e: e.scalar_tensor_tensor(
                out=stage_l[:, slot, :], in0=bank, scalar=bias[:, g:g + 1],
                in1=stage_h[:, slot, :].bitcast(F32), op0=ALU.add, op1=ALU.subtract))
            free[bank_name] = [high, low]
            return slot, projected, high, low

        def stack(slot, high, low, parts, dst):
            sp.wait(high, low)
            for j in range(QUAD):
                for r, part in enumerate(parts):
                    src = stage_h if part == "h" else stage_l
                    def start(e, j=j, r=r, src=src):
                        return e.dma_start(dst(j)[r * DK:(r + 1) * DK, :].bitcast(F32),
                                           src[j * DK:(j + 1) * DK, slot, :].bitcast(F32))
                    stage_land[slot].dma(sp, start)
            return stage_land[slot].mark()

        xT_ready, q_staged, q_ready = {}, {}, {}
        scores2_done = {}
        score1_done = {}

        def load_xT(chunk):
            b, k = divmod(chunk, NC)
            i = chunk % 2
            sp.wait(*released(f"xT{i}"))
            land[f"xT{i}"].dma(sp, lambda e: e.dma_start(
                xT_sb[:, i, :, :], xT[b, :, k * CH:(k + 1) * CH].rearrange("(t p) n -> p t n", p=P)))
            xT_ready[chunk] = land[f"xT{i}"].mark()

        def project_q(unit):
            chunk, g = divmod(unit, G)
            pe.wait(land["wq"].mark(), xT_ready[chunk])
            slot, projected, high, low = project_split(
                wq, bq_col, xT_sb[:, chunk % 2, :, :], g, misc[:, 0:CH], "misc", land_cols)
            q_staged[unit] = slot, high, low
            if g == G - 1:
                free[f"xT{chunk % 2}"] = [projected]
                if chunk + 2 < B * NC:
                    load_xT(chunk + 2)

        def stack_q(unit):
            slot, high, low = q_staged[unit]
            i = unit % NQ
            sp.wait(*released(f"q_stack{i}"))
            q_ready[unit] = stack(slot, high, low, "hhl", lambda j: q_stack[:, i, j, :])

        land_cols = land["cols"].mark()
        land_rows = land["rows"].mark()

        k_ready, v_ready, kv_ready = {}, {}, {}
        spare = [("score0", score[0]), ("score1", score[1]), ("acc", acc), ("misc", misc)]

        def keys_and_values(b, fill):
            for name, dst, src in (("wk", wk, WkT), ("wv", wv, WvT)):
                sp.wait(*released("p_ring"))
                land[name].dma(sp, lambda e, d=dst, s=src: e.dma_start(
                    d, s.rearrange("(t p) n -> p t n", p=P)))
            wk_ready, wv_ready = land["wk"].mark(), land["wv"].mark()
            n = 0
            for k in range(NC):
                i = k % 2
                sp.wait(*released("p_ring"), *released(f"ctxT{i}"))
                land[f"ctxT{i}"].dma(sp, lambda e: e.dma_start(
                    ctxT_sb[i], ctxT[b, :, k * CH:(k + 1) * CH].rearrange("(t p) n -> p t n", p=P)))
                loaded = land[f"ctxT{i}"].mark()
                for g in range(G):
                    pe.wait(wk_ready, loaded)
                    name, bank = spare[n % len(spare)]
                    n += 1
                    slot, _, high, low = project_split(
                        wk, bk_col, ctxT_sb[i], g, bank[:, 0:CH], name, land_cols)
                    sp.wait(*released("k_stack"))
                    stack(slot, high, low, "hlh",
                          lambda j: k_stack[:, g * QUAD + j, k * CH:(k + 1) * CH])
                    fill()
                for t in range(TPC):
                    name, bank = spare[n % len(spare)]
                    n += 1
                    pe.wait(wv_ready, *released(name))
                    for f in range(G):
                        step = lambda e, f=f: e.matmul(bank[:], ctxT_sb[i][:, f, t * P:(t + 1) * P],
                                                       wv[:, f, :], start=f == 0, stop=f == G - 1)
                        pe.do(step) if f < G - 1 else None
                    projected = pe.mark(step)
                    dve.wait(projected, land_rows, *released("v_sb"))
                    v_ready[b] = dve.mark(lambda e: e.tensor_tensor(
                        v_sb[:, k * TPC + t, :], bank[:], rows_sb["bv"][:], ALU.add))
                    free[name] = [v_ready[b]]
                    fill()
                free[f"ctxT{i}"] = [projected]
            k_ready[b] = [landing.mark() for landing in stage_land]
            for name in ("ctxT0", "ctxT1"):
                free["p_ring"] = free.get("p_ring", []) + [projected]

        def elu(src, src_ready, e_tile, e_name, dst, dst_name):
            dve.wait(*src_ready, *released(e_name))
            low = dve.mark(lambda e: e.tensor_scalar(e_tile, src, 0.0, None, ALU.min))
            act.wait(low)
            grown = act.mark(lambda e: e.activation(e_tile, e_tile, ACT.Exp))
            dve.wait(grown)
            less = dve.mark(lambda e: e.tensor_scalar(e_tile, e_tile, -1.0, None, ALU.add))
            dve.wait(less, *released(dst_name))
            done = dve.mark(lambda e: e.scalar_tensor_tensor(
                out=dst, in0=src, scalar=0.0, in1=e_tile, op0=ALU.max, op1=ALU.add))
            free[e_name] = [done]
            return done

        def linear_sums(b):
            banks = [scoreT[d // 2][:, (d % 2) * HALF:(d % 2 + 1) * HALF] for d in range(G)]
            phi = [phi_sb[:], phiT_sb[:]]
            names = ["phi", "phiT"]
            for t in range(KT):
                i = t % 2
                sp.wait(*released("p_ring"), *released(f"ctx_nat{i}"))
                land[f"ctx_nat{i}"].dma(sp, lambda e: e.dma_start(
                    ctx_nat[i], ctx[b, t * P:(t + 1) * P, :]))
                loaded = land[f"ctx_nat{i}"].mark()
                done = elu(ctx_nat[i], [loaded], e_sb[:, i, :], f"e{i}", phi[i], names[i])
                pe.wait(done, loaded, ones_ready, *released("scoreT0"), *released("scoreT1"), *released("score0"))
                for d in range(G):
                    pe.do(lambda e, d=d: e.matmul(banks[d], phi[i][:, d * P:(d + 1) * P], ctx_nat[i],
                                                  start=t == 0, stop=t == KT - 1))
                summed = pe.mark(lambda e: e.matmul(score[0][:], ones[:], phi[i],
                                                    start=t == 0, stop=t == KT - 1))
                free[names[i]] = [summed]
                free[f"ctx_nat{i}"] = [summed]
            act.wait(summed, *released("kv"))
            dve.wait(summed, *released("kv"))
            kept = [act.mark(lambda e, d=d: e.activation(kv_sb[:, d, :], banks[d], ACT.Copy))
                    for d in range(G)]
            sums = dve.mark(lambda e: e.tensor_copy(ksum_sb[:], score[0][:]))
            free["scoreT0"], free["scoreT1"], free["score0"] = [kept[1]], [kept[3]], [sums]
            free["ctx_nat"] = [summed]
            kv_ready[b] = [kept[3], sums]
            return summed

        n_score = [0]
        shift_ready = {}
        maxed = {}

        def pass1(b, unit, i):
            j, t = divmod(i, TPC)
            g = unit % G
            for h in range(S // HALF):
                slot = n_score[0] % 2
                n_score[0] += 1
                pe.wait(q_ready[unit], *k_ready[b], *released(f"score{slot}"))
                scored = pe.mark(lambda e, h=h, slot=slot: e.matmul(
                    score[slot][:], q_stack[0:SPLIT, unit % NQ, j, t * P:(t + 1) * P],
                    k_stack[0:SPLIT, g * QUAD + j, h * HALF:(h + 1) * HALF], start=True, stop=True))
                dve.wait(scored, *released(f"maxes{unit % 2}"))
                maxed[unit] = dve.mark(lambda e, h=h, slot=slot: e.reduce_max(
                    maxes[:, unit % 2, h, t, j:j + 1], score[slot][:], AX.X))
                free[f"score{slot}"] = [maxed[unit]]

        def split_max(unit):
            u = unit % 2
            dve.wait(maxed[unit])
            whole = dve.mark(lambda e: e.tensor_tensor(max_row[:], maxes[:, u, 0], maxes[:, u, 1], ALU.max))
            free[f"maxes{u}"] = [whole]
            dve.wait(whole, *released(f"neg_max{u}"))
            high = dve.mark(lambda e: e.tensor_scalar(
                neg_max[:, u, :, 0:QUAD], max_row[:], -1.0, None, ALU.mult))
            dve.wait(high)
            return dve.mark(lambda e: e.scalar_tensor_tensor(
                out=neg_max[:, u, :, QUAD:2 * QUAD], in0=max_row[:], scalar=-1.0,
                in1=neg_max[:, u, :, 0:QUAD].bitcast(F32), op0=ALU.mult, op1=ALU.subtract))

        def place_max(unit, split):
            u, slot = unit % 2, n_score[0] % 2
            n_score[0] += 1
            pe.wait(split, ident_ready, *released(f"score{slot}"))
            for t in range(TPC):
                step = lambda e, t=t: e.matmul(
                    score[slot][SPLIT:ROWS, t * P:(t + 1) * P], neg_max[:, u, t, :].bitcast(F32), ident[:],
                    start=True, stop=True, tile_position=(0, SPLIT))
                pe.do(step) if t < TPC - 1 else None
            turned = pe.mark(step)
            free[f"neg_max{u}"] = [turned]
            act.wait(turned, *released(f"q_stack{unit % NQ}"))
            shift_ready[unit] = act.mark(lambda e: e.activation(
                q_stack[SPLIT:ROWS, unit % NQ, :, :],
                score[slot][SPLIT:ROWS, 0:CH].unsqueeze(1).to_broadcast([2 * QUAD, QUAD, CH]), ACT.Copy))
            free[f"score{slot}"] = [shift_ready[unit]]

        exped = {}
        paired = {}
        quads = {}
        p_free = {}

        def pass2(b, unit, kt, n):
            g, i = unit % G, n % 2
            pe.wait(shift_ready[unit], hot_ready, *released(f"scoreT{i}"))
            for j in range(QUAD):
                step = lambda e, j=j: e.matmul(
                    scoreT[i][:, j * CH:(j + 1) * CH],
                    k_stack[0:ROWS, g * QUAD + j, kt * P:(kt + 1) * P],
                    q_stack[0:ROWS, unit % NQ, j, :], start=True, stop=True)
                pe.do(step) if j < QUAD - 1 else None
            scored = pe.mark(step)
            scores2_done[unit] = scored
            free[f"q_stack{unit % NQ}"] = [scored]
            act.wait(scored, *p_free.get(n - NP, released("ctx_nat")))
            exped[n] = act.mark(lambda e: e.activation(
                p_ring[:, n % NP, :], scoreT[i][:], ACT.Exp, scale=SCALE))
            free[f"scoreT{i}"] = [exped[n]]

        def add_pair(n):
            i = (n // 2) % 2
            pool.wait(exped[n], *released(f"pair{i}"))
            paired[n // 2] = pool.mark(lambda e: e.tensor_tensor(
                pair_sum[:, i, :], p_ring[:, (n - 1) % NP, :], p_ring[:, n % NP, :], ALU.add))

        def add_quad(n):
            dve.wait(paired[n // 2], *released("quad"))
            quads[n // 4] = dve.mark(lambda e: e.tensor_tensor(
                quad_sum[:], pair_sum[:, 0, :], pair_sum[:, 1, :], ALU.add))
            free["pair0"] = free["pair1"] = [quads[n // 4]]

        def value_product(b, unit, kt, n):
            pe.wait(exped[n], v_ready[b])
            if kt == 0:
                pe.wait(*released("acc"))
            for j in range(QUAD):
                head = (unit % G) * QUAD + j
                step = lambda e, j=j, head=head: e.matmul(
                    acc[j * DK:(j + 1) * DK, 0:CH], v_sb[:, kt, head * DK:(head + 1) * DK],
                    p_ring[:, n % NP, j * CH:(j + 1) * CH], start=kt == 0, stop=kt == KT - 1,
                    tile_position=(0, j * DK), skip_group_check=True)
                pe.do(step) if j < QUAD - 1 else None
            used = pe.mark(step)
            p_free[n] = [used, paired[n // 2]]
            return used

        def denominator(unit, n, first, last):
            pe.wait(quads[n // 4], ones_ready)
            for j in range(QUAD):
                step = lambda e, j=j: e.matmul(
                    acc[j * DK:(j + 1) * DK, CH:2 * CH], ones[:, 0:DK], quad_sum[:, j * CH:(j + 1) * CH],
                    start=False, stop=last, tile_position=(0, j * DK), skip_group_check=True)
                pe.do(step) if j < QUAD - 1 else None
            summed = pe.mark(step)
            free["quad"] = [summed]
            return summed

        out_done = {}

        def normalise(b, unit, summed):
            chunk, g = b * NC + unit // G % NC, unit % G
            i = chunk % 2
            dve.wait(summed, *released(f"outT{i}"))
            inverse = dve.mark(lambda e: e.reciprocal(outT[:, i, g, :], acc[:, CH:2 * CH]))
            dve.wait(inverse)
            out_done[chunk] = dve.mark(lambda e: e.tensor_tensor(
                outT[:, i, g, :], acc[:, 0:CH], outT[:, i, g, :], ALU.mult))
            free["acc"] = [out_done[chunk]]

        def layer_norm(src, ready, gamma, beta, scratch, scratch_name, dst, dst_name):
            dve.wait(ready, *released("stats"))
            counted = dve.mark(lambda e: e.bn_stats(stats[:], src))
            dve.wait(counted, *released("mean_var"))
            aggregated = dve.mark(lambda e: e.bn_aggr(mean_var[:], stats[:]))
            dve.wait(aggregated, *released("var_eps"))
            added = dve.mark(lambda e: e.tensor_scalar(var_eps[:], mean_var[:, 1:2], LN_EPS, None, ALU.add))
            pool.wait(added, half_ready, *released("rstd"))
            root = pool.mark(lambda e: e.tensor_tensor(rstd[:], var_eps[:], minus_half[:], ALU.pow))
            free["var_eps"] = [root]
            yield
            dve.wait(root, *released(scratch_name))
            normal = dve.mark(lambda e: e.tensor_scalar(
                scratch, src, mean_var[:, 0:1], rstd[:], ALU.subtract, ALU.mult))
            free["mean_var"] = free["rstd"] = [normal]
            pool.wait(normal)
            scaled = pool.mark(lambda e: e.tensor_tensor(scratch, scratch, rows_sb[gamma][:], ALU.mult))
            pool.wait(scaled, *released(dst_name))
            yield pool.mark(lambda e: e.tensor_tensor(dst, scratch, rows_sb[beta][:], ALU.add))

        n_nat = [0]

        def finish_chunk(chunk):
            b, k = divmod(chunk, NC)
            for t in range(TPC):
                token = k * CH + t * P
                i = n_nat[0] % 2
                n_nat[0] += 1
                sp.wait(*released(f"x_nat{i}"))
                land[f"x_nat{i}"].dma(sp, lambda e: e.dma_start(x_nat[:, i, :], x[b, token:token + P, :]))
                loaded = land[f"x_nat{i}"].mark()
                pool.wait(loaded, land_rows)
                biased = pool.mark(lambda e: e.tensor_tensor(
                    x_nat[:, i, :], x_nat[:, i, :], rows_sb["bo"][:], ALU.add))
                yield
                pe.wait(out_done[chunk], land["wo"].mark(), *released("misc"))
                for g in range(G):
                    step = lambda e, g=g: e.matmul(misc[:], outT[:, chunk % 2, g, t * P:(t + 1) * P],
                                                   wo[:, g, :], start=g == 0, stop=g == G - 1)
                    pe.do(step) if g < G - 1 else None
                projected = pe.mark(step)
                free[f"outT{chunk % 2}"] = [projected]
                dve.wait(projected, biased, *released("y"))
                y = dve.mark(lambda e: e.tensor_tensor(y_sb[:], misc[:], x_nat[:, i, :], ALU.add))
                free["misc"] = [y]
                free[f"x_nat{i}"] = [y]
                yield
                x1 = None
                for x1 in layer_norm(y_sb[:], y, "gamma0", "beta0", y_sb[:], "-", x1_sb[:], "x1"):
                    yield
                free["y"] = [x1]
                phi = elu(x1_sb[:], [x1], e_sb[:, 0, :], "e0", phi_sb[:], "phi")
                dve.wait(phi, *kv_ready[b])
                dotted = dve.mark(lambda e: e.tensor_tensor_reduce(
                    out=e_sb[:, 1, :], in0=phi_sb[:], in1=ksum_sb[:], scale=1.0, scalar=0.0,
                    op0=ALU.mult, op1=ALU.add, accum_out=z_sb[:, 0:1]))
                dve.wait(dotted)
                shifted = dve.mark(lambda e: e.tensor_scalar(z_sb[:, 1:2], z_sb[:, 0:1], ATTN_EPS, None, ALU.add))
                dve.wait(shifted)
                z = dve.mark(lambda e: e.reciprocal(z_sb[:, 2:3], z_sb[:, 1:2]))
                yield
                yield
                pe.wait(phi, ident_ready, *released("misc"))
                for d in range(G):
                    step = lambda e, d=d: e.matmul(
                        misc[:, d * P:(d + 1) * P], phi_sb[:, d * P:(d + 1) * P], ident[:],
                        start=True, stop=True, is_transpose=True)
                    pe.do(step) if d < G - 1 else None
                turned = pe.mark(step)
                free["phi"] = [turned, dotted]
                act.wait(turned, *released("phiT"))
                kept = act.mark(lambda e: e.activation(phiT_sb[:], misc[:], ACT.Copy))
                free["misc"] = [kept]
                yield
                pe.wait(kept, *kv_ready[b], *released("misc"))
                for d in range(G):
                    step = lambda e, d=d: e.matmul(misc[:], phiT_sb[:, d * P:(d + 1) * P], kv_sb[:, d, :],
                                                   start=d == 0, stop=d == G - 1)
                    pe.do(step) if d < G - 1 else None
                attended = pe.mark(step)
                free["phiT"] = [attended]
                free["kv"] = [attended, dotted]
                dve.wait(attended, z, x1, *released("y"))
                y = dve.mark(lambda e: e.scalar_tensor_tensor(
                    out=y_sb[:], in0=misc[:], scalar=z_sb[:, 2:3], in1=x1_sb[:], op0=ALU.mult, op1=ALU.add))
                free["misc"] = [y]
                free["x1"] = [y]
                yield
                for result in layer_norm(y_sb[:], y, "gamma1", "beta1", y_sb[:], "-", x_nat[:, i, :], f"x_nat{i}"):
                    yield
                free["y"] = [result]
                sp.wait(result)
                land[f"out{i}"].dma(sp, lambda e: e.dma_start(out[b, token:token + P, :], x_nat[:, i, :]))
                free[f"x_nat{i}"] = [land[f"out{i}"].mark()]
                yield

        background = []

        def fill():
            while background:
                try:
                    next(background[0])
                    return
                except StopIteration:
                    background.pop(0)

        load_xT(0)
        load_xT(1)
        for unit in range(NQ):
            project_q(unit)
            stack_q(unit)
        for b in range(B):
            keys_and_values(b, fill)
            while background:
                fill()
            linear_sums(b)
            first = b * UNITS
            total = UNITS * STEPS
            splits = {}
            def pass1_step(m):
                if m < total:
                    pass1(b, first + m // STEPS, m % STEPS)
                    if m % STEPS == STEPS - 1:
                        splits[m // STEPS] = split_max(first + m // STEPS)
                if m % STEPS == 0 and 0 < m <= total:
                    place_max(first + m // STEPS - 1, splits[m // STEPS - 1])
            for m in range(STEPS + LEAD):
                pass1_step(m)
            last_value = None
            for n in range(total + LAG + 4):
                unit, kt = first + n // STEPS, n % STEPS
                if n < total:
                    pass2(b, unit, kt, n)
                q = n - 3
                if q % 4 == 3 and 0 <= q < total:
                    add_quad(q)
                q = n - 1
                if q % 2 and 0 < q < total:
                    add_pair(q)
                q = n - LAG
                if 0 <= q < total:
                    last_value = value_product(b, first + q // STEPS, q % STEPS, q)
                q = n - 5 
                if q % 4 == 3 and 0 <= q < total:
                    end = q % STEPS == STEPS - 1
                    summed = denominator(first + q // STEPS, q, q % STEPS == 3, end)
                    sums_done = summed
                q = n - LAG
                if q % STEPS == STEPS - 1 and 0 <= q < total:
                    normalise(b, q // STEPS, last_value)
                    if (q // STEPS) % G == G - 1:
                        background.append(finish_chunk(b * NC + q // STEPS // G))
                pass1_step(n + STEPS + LEAD)
                fresh = unit + NQ
                if n < total and fresh < B * UNITS:
                    if kt == 4:
                        project_q(fresh)
                    if kt == STEPS - 1:
                        stack_q(fresh)
                fill()
            free["k_stack"] = [scores2_done[first + UNITS - 1]]
            free["v_sb"] = [last_value]
            free["p_ring"] = [last_value, paired[total // 2 - 1]]
            free["ctx_nat"] = []
            p_free.clear()
        while background:
            fill()
        sp.wait(land["out0"].mark(), land["out1"].mark())


def kernel(x, ctx_1024, L0_xattn_Wq, L0_xattn_bq, L0_xattn_Wk, L0_xattn_bk, L0_xattn_Wv, L0_xattn_bv,
           L0_xattn_Wo, L0_xattn_bo, L0_xattn_gamma, L0_xattn_beta, L1_xattn_gamma, L1_xattn_beta):
    import numpy as np
    import concourse.bacc as bacc
    from concourse.bass_utils import run_bass_kernel_spmd

    def turned(a):
        return np.ascontiguousarray(np.swapaxes(np.asarray(a), -1, -2))

    ins = {
        "x_in": x, "xT_in": turned(x), "ctx_in": ctx_1024, "ctxT_in": turned(ctx_1024),
        "WqT_in": turned(L0_xattn_Wq), "bq_in": L0_xattn_bq, "WkT_in": turned(L0_xattn_Wk), "bk_in": L0_xattn_bk,
        "WvT_in": turned(L0_xattn_Wv), "bv_in": L0_xattn_bv, "WoT_in": turned(L0_xattn_Wo), "bo_in": L0_xattn_bo,
        "gamma0_in": L0_xattn_gamma, "beta0_in": L0_xattn_beta,
        "gamma1_in": L1_xattn_gamma, "beta1_in": L1_xattn_beta,
    }
    nc = bacc.Bacc("TRN2", target_bir_lowering=False, num_devices=1)
    arrays = {n: np.ascontiguousarray(a) for n, a in ins.items()}
    aps = [nc.dram_tensor(n, a.shape, mybir.dt.from_np(a.dtype), kind="ExternalInput").ap() for n, a in arrays.items()]
    res = nc.dram_tensor("res_out", arrays["x_in"].shape, F32, kind="ExternalOutput").ap()
    build(nc, *aps, res)
    return run_bass_kernel_spmd(nc, [arrays], core_ids=[0]).results[0]["res_out"]
```

```python
from contextlib import ExitStack

import concourse.bass as bass
from concourse import mybir

F32 = mybir.dt.float32
F32R = mybir.dt.float32r
ALU = mybir.AluOpType
ACT = mybir.ActivationFunctionType
AX = mybir.AxisListType


class Stream:

    def __init__(self, engine, sem):
        self.engine, self.sem, self.count, self.seen = engine, sem, 0, {}

    def wait(self, *marks):
        for sem, value in marks:
            if self.seen.get(id(sem), 0) < value:
                self.seen[id(sem)] = value
                self.engine.wait_ge(sem, value)

    def do(self, instruction):
        instruction(self.engine)

    def mark(self, instruction):
        self.count += 1
        instruction(self.engine).then_inc(self.sem, 1)
        return self.sem, self.count


class Landing:

    def __init__(self, sem):
        self.sem, self.count = sem, 0

    def dma(self, stream, start):
        self.count += 16
        stream.do(lambda e: start(e).then_inc(self.sem, 16))

    def mark(self):
        return self.sem, self.count


def build(nc, x, xT, ctx, ctxT, WqT, bq, WkT, bk, WvT, bv, WoT, bo, gamma0, beta0, gamma1, beta1, out):
    B, S, D = x.shape
    P = nc.NUM_PARTITIONS
    DK = 32
    QUAD = P // DK
    G = D // P
    CH = 256
    NC = S // CH
    TPC = CH // P
    KT = S // P
    STEPS = KT
    HALF = 512
    SCALE = float(DK) ** -0.5
    LN_EPS, ATTN_EPS = 1e-5, 1e-6
    LEAD = 3
    LAG = 6
    NQ, NP, NSTAGE = 3, 7, 2
    SPLIT = 3 * DK
    ROWS = SPLIT + 2 * QUAD
    UNITS = NC * G

    with ExitStack() as c:
        def sb(name, shape, dt=F32):
            return c.enter_context(nc.sbuf_tensor(name, shape, dt))

        def ps(name, cols):
            return c.enter_context(nc.psum_tensor(name, [P, cols], F32))

        def sem(name):
            return c.enter_context(nc.semaphore(name))

        wq = sb("wq", [P, G, D])
        wo = sb("wo", [P, G, D])
        k_stack = sb("k_stack", [P, G * QUAD, S], F32R)
        q_stack = sb("q_stack", [P, NQ, QUAD, CH], F32R)
        v_sb = sb("v_sb", [P, KT, D])
        xT_sb = sb("xT_sb", [P, 2, G, CH])
        stage_h = sb("stage_h", [P, NSTAGE, CH], F32R)
        stage_l = sb("stage_l", [P, NSTAGE, CH], F32R)
        outT = sb("outT", [P, 2, G, CH])
        kv_sb = sb("kv_sb", [P, G, D])
        ksum_sb = sb("ksum_sb", [P, D])
        x_nat = sb("x_nat", [P, 2, D])
        y_sb = sb("y_sb", [P, D])
        x1_sb = sb("x1_sb", [P, D])
        e_sb = sb("e_sb", [P, 2, D])
        phi_sb = sb("phi_sb", [P, D])
        phiT_sb = sb("phiT_sb", [P, D])
        rows_sb = {n: sb(n + "_row", [P, D]) for n in ("bv", "bo", "gamma0", "beta0", "gamma1", "beta1")}
        bq_col = sb("bq_col", [P, G])
        bk_col = sb("bk_col", [P, G])
        ident = sb("ident", [P, P])
        ones = sb("ones", [P, P])
        onehot = sb("onehot", [P, QUAD])
        maxes = sb("maxes", [P, 2, 2, TPC, QUAD])
        max_row = sb("max_row", [P, TPC, QUAD])
        neg_max = sb("neg_max", [P, 2, TPC, 2 * QUAD], F32R)
        stats = sb("stats", [P, 6])
        mean_var = sb("mean_var", [P, 2])
        var_eps = sb("var_eps", [P, 1])
        rstd = sb("rstd", [P, 1])
        minus_half = sb("minus_half", [P, 1])
        z_sb = sb("z_sb", [P, 3])
        den_inverse = sb("den_inverse", [P, CH // DK])
        with ExitStack() as early:
            def sb_early(name, shape, dt=F32):
                return early.enter_context(nc.sbuf_tensor(name, shape, dt))

            wk = sb_early("wk", [P, G, D])
            wv = sb_early("wv", [P, G, D])
            ctxT_sb = sb_early("ctxT_sb", [P, G, S])
            k_high = sb_early("k_high", [P, HALF], F32R)
            k_low = sb_early("k_low", [P, HALF], F32R)
        p_ring = sb("p_ring", [P, NP, QUAD * CH])
        pair_sum = sb("pair_sum", [P, 2, QUAD * CH])
        quad_sum = sb("quad_sum", [P, QUAD * CH])
        scoreT = [ps(f"scoreT{i}", HALF) for i in range(3)]
        score = [ps(f"score{i}", HALF) for i in range(3)]
        acc = ps("acc", HALF)
        misc = ps("misc", HALF)

        pe, act, dve, pool, sp = (Stream(engine, sem(name)) for engine, name in (
            (nc.tensor, "pe"), (nc.scalar, "act"), (nc.vector, "dve"), (nc.gpsimd, "pool"), (nc.sync, "sp")))
        land = {n: Landing(sem("dma_" + n)) for n in
                ("wq", "wo", "wk", "wv", "rows", "cols", "xT0", "xT1", "ctxT0", "ctxT1",
                 "x_nat0", "x_nat1", "out0", "out1")}
        free = {}

        def released(name):
            return free.get(name, [])

        for name, src in (("bv", bv), ("bo", bo), ("gamma0", gamma0), ("beta0", beta0),
                          ("gamma1", gamma1), ("beta1", beta1)):
            land["rows"].dma(sp, lambda e, n=name, s=src: e.dma_start(
                rows_sb[n][:], s.partition_broadcast(P)))
        for dst, src in ((bq_col, bq), (bk_col, bk)):
            land["cols"].dma(sp, lambda e, d=dst, s=src: e.dma_start(
                d[:], s.rearrange("(t p) -> p t", p=P), allow_slow_non_contiguous=True))
        land["wq"].dma(sp, lambda e: e.dma_start(wq[:], WqT.rearrange("(t p) n -> p t n", p=P)))
        land["wo"].dma(sp, lambda e: e.dma_start(wo[:], WoT.rearrange("(t p) n -> p t n", p=P)))

        cleared = pool.mark(lambda e: e.memset(ident[:], 0.0))
        hot_cleared = pool.mark(lambda e: e.memset(onehot[:], 0.0))
        pool.wait(cleared)
        ident_ready = pool.mark(lambda e: e.affine_select(
            out=ident[:], in_=ident[:], compare_op=ALU.not_equal, fill=1.0, base=0,
            pattern=[[-1, P]], channel_multiplier=1))
        hot = hot_cleared
        for r in range(2):
            pool.wait(hot)
            hot = pool.mark(lambda e, r=r: e.affine_select(
                out=onehot[:], in_=onehot[:], compare_op=ALU.not_equal, fill=1.0,
                base=-(SPLIT + r * QUAD), pattern=[[-1, QUAD]], channel_multiplier=1))
        ones_ready = pool.mark(lambda e: e.memset(ones[:], 1.0))
        half_ready = pool.mark(lambda e: e.memset(minus_half[:], -0.5))
        dve.wait(hot)
        for g in range(G):
            hot_ready = dve.mark(lambda e, g=g: e.tensor_copy(
                k_stack[SPLIT:ROWS, g * QUAD:(g + 1) * QUAD, :],
                onehot[SPLIT:ROWS, :].unsqueeze(2).to_broadcast([2 * QUAD, QUAD, S])))

        n_stage = [0]
        stage_land = [Landing(sem(f"dma_stage{i}")) for i in range(NSTAGE + 1)]

        def project_split(weight, bias, src, g, bank, bank_name, high_out, low_out, landed):
            pe.wait(*released(bank_name))
            for t in range(G):
                step = lambda e, t=t: e.matmul(bank, weight[:, t, g * P:(g + 1) * P], src[:, t, :],
                                               start=t == 0, stop=t == G - 1)
                pe.do(step) if t < G - 1 else None
            projected = pe.mark(step)
            act.wait(projected, land_cols, *landed)
            high = act.mark(lambda e: e.activation(high_out, bank, ACT.Identity, bias=bias[:, g:g + 1]))
            dve.wait(projected, high, *landed)
            low = dve.mark(lambda e: e.scalar_tensor_tensor(
                out=low_out, in0=bank, scalar=bias[:, g:g + 1], in1=high_out.bitcast(F32),
                op0=ALU.add, op1=ALU.subtract))
            free[bank_name] = [high, low]
            return projected, high, low

        def stack(high_src, low_src, high, low, parts, dst, landing):
            sp.wait(high, low)
            for j in range(QUAD):
                for r, part in enumerate(parts):
                    src = high_src if part == "h" else low_src
                    landing.dma(sp, lambda e: e.dma_start(
                        dst(j)[r * DK:(r + 1) * DK, :].bitcast(F32), src[j * DK:(j + 1) * DK, :].bitcast(F32)))
            return landing.mark()

        xT_ready, q_staged, q_ready = {}, {}, {}
        scores2_done = {}
        score1_done = {}

        def load_xT(chunk):
            b, k = divmod(chunk, NC)
            i = chunk % 2
            sp.wait(*released(f"xT{i}"))
            land[f"xT{i}"].dma(sp, lambda e: e.dma_start(
                xT_sb[:, i, :, :], xT[b, :, k * CH:(k + 1) * CH].rearrange("(t p) n -> p t n", p=P)))
            xT_ready[chunk] = land[f"xT{i}"].mark()

        def project_q(unit):
            chunk, g = divmod(unit, G)
            pe.wait(land["wq"].mark(), xT_ready[chunk])
            slot = n_stage[0] % NSTAGE
            n_stage[0] += 1
            projected, high, low = project_split(
                wq, bq_col, xT_sb[:, chunk % 2, :, :], g, misc[:, 0:CH], "misc",
                stage_h[:, slot, :], stage_l[:, slot, :],
                [stage_land[slot].mark(), stage_land[0].mark()])
            q_staged[unit] = slot, high, low
            if g == G - 1:
                free[f"xT{chunk % 2}"] = [projected]
                if chunk + 2 < B * NC:
                    load_xT(chunk + 2)

        def stack_q(unit):
            slot, high, low = q_staged[unit]
            i = unit % NQ
            sp.wait(*released(f"q_stack{i}"))
            q_ready[unit] = stack(stage_h[:, slot, :], stage_l[:, slot, :], high, low, "hhl",
                                  lambda j: q_stack[:, i, j, :], stage_land[slot])

        land_cols = land["cols"].mark()
        land_rows = land["rows"].mark()

        k_ready, v_ready, kv_ready = {}, {}, {}
        spare = [("score0", score[0]), ("score1", score[1]), ("score2", score[2]), ("misc", misc)]

        def keys_and_values(b, fill):
            sp.wait(*released("p_ring"))
            land["wk"].dma(sp, lambda e: e.dma_start(wk[:], WkT.rearrange("(t p) n -> p t n", p=P)))
            loaded = []
            for h in range(S // HALF):
                cols = slice(h * HALF, (h + 1) * HALF)
                land[f"ctxT{h}"].dma(sp, lambda e: e.dma_start(
                    ctxT_sb[:, :, cols], ctxT[b, :, cols].rearrange("(t p) n -> p t n", p=P)))
                loaded.append(land[f"ctxT{h}"].mark())
                if h == 0:
                    land["wv"].dma(sp, lambda e: e.dma_start(wv[:], WvT.rearrange("(t p) n -> p t n", p=P)))
            n = 0
            for g in range(G):
                for h in range(S // HALF):
                    name, bank = spare[n % len(spare)]
                    n += 1
                    if h == 0:
                        high_out, low_out = (s[:].rearrange("p a n -> p (a n)") for s in (stage_h, stage_l))
                        landing, landed = stage_land[0], [stage_land[0].mark(), stage_land[1].mark()]
                    else:
                        high_out, low_out = k_high[:], k_low[:]
                        landing, landed = stage_land[2], [stage_land[2].mark(), *released("p_ring")]
                    pe.wait(land["wk"].mark(), loaded[h])
                    _, high, low = project_split(wk, bk_col, ctxT_sb[:, :, h * HALF:(h + 1) * HALF], g,
                                                 bank[:], name, high_out, low_out, landed)
                    sp.wait(*released("k_stack"))
                    k_ready[b] = k_ready.get(b, []) + [
                        stack(high_out, low_out, high, low, "hlh",
                              lambda j: k_stack[:, g * QUAD + j, h * HALF:(h + 1) * HALF], landing)]
                    fill()
                for t in range(g * KT // G, (g + 1) * KT // G):
                    name, bank = spare[n % len(spare)]
                    n += 1
                    pe.wait(land["wv"].mark(), *loaded, *released(name))
                    for f in range(G):
                        step = lambda e, f=f: e.matmul(bank[:], ctxT_sb[:, f, t * P:(t + 1) * P],
                                                       wv[:, f, :], start=f == 0, stop=f == G - 1)
                        pe.do(step) if f < G - 1 else None
                    projected = pe.mark(step)
                    dve.wait(projected, land_rows, *released("v_sb"))
                    v_ready[b] = dve.mark(lambda e: e.tensor_tensor(
                        v_sb[:, t, :], bank[:], rows_sb["bv"][:], ALU.add))
                    free[name] = [v_ready[b]]
                    fill()
            free["early"] = [projected, *k_ready[b]]

        def elu(src, src_ready, e_tile, e_name, dst, dst_name):
            dve.wait(*src_ready, *released(e_name))
            low = dve.mark(lambda e: e.tensor_scalar(e_tile, src, 0.0, None, ALU.min))
            act.wait(low)
            grown = act.mark(lambda e: e.activation(e_tile, e_tile, ACT.Exp))
            yield
            dve.wait(grown)
            less = dve.mark(lambda e: e.tensor_scalar(e_tile, e_tile, -1.0, None, ALU.add))
            dve.wait(less, *released(dst_name))
            done = dve.mark(lambda e: e.scalar_tensor_tensor(
                out=dst, in0=src, scalar=0.0, in1=e_tile, op0=ALU.max, op1=ALU.add))
            free[e_name] = [done]
            yield done

        def linear_sums(b):
            banks = [scoreT[0], scoreT[1], scoreT[2], acc]
            phi = [phi_sb[:], phiT_sb[:]]
            names = ["phi", "phiT"]
            for t in range(KT):
                i = t % 2
                sp.wait(*released(f"x_nat{i}"))
                ctx_nat = x_nat[:, i, :]
                land[f"x_nat{i}"].dma(sp, lambda e: e.dma_start(ctx_nat, ctx[b, t * P:(t + 1) * P, :]))
                loaded = land[f"x_nat{i}"].mark()
                *_, done = elu(ctx_nat, [loaded], e_sb[:, i, :], f"e{i}", phi[i], names[i])
                pe.wait(done, loaded, ones_ready, *released("score0"),
                        *released("scoreT0"), *released("scoreT1"), *released("scoreT2"), *released("acc"))
                for d in range(G):
                    pe.do(lambda e, d=d: e.matmul(banks[d][:], phi[i][:, d * P:(d + 1) * P], ctx_nat,
                                                  start=t == 0, stop=t == KT - 1))
                summed = pe.mark(lambda e: e.matmul(score[0][:], ones[:], phi[i],
                                                    start=t == 0, stop=t == KT - 1))
                free[names[i]] = [summed]
                free[f"x_nat{i}"] = [summed]
            act.wait(summed, *released("kv"))
            dve.wait(summed, *released("kv"))
            kept = [act.mark(lambda e, d=d: e.activation(kv_sb[:, d, :], banks[d][:], ACT.Copy))
                    for d in range(G)]
            sums = dve.mark(lambda e: e.tensor_copy(ksum_sb[:], score[0][:]))
            for name, mark in zip(("scoreT0", "scoreT1", "scoreT2", "acc", "score0"), (*kept, sums)):
                free[name] = [mark]
            kv_ready[b] = [kept[3], sums]
            return summed

        n_score = [0]
        shift_ready = {}
        maxed = {}

        def pass1(b, unit, i):
            j, t = divmod(i, TPC)
            g = unit % G
            for h in range(S // HALF):
                slot = n_score[0] % 3
                n_score[0] += 1
                pe.wait(q_ready[unit], *k_ready[b], *released(f"score{slot}"))
                scored = pe.mark(lambda e, h=h, slot=slot: e.matmul(
                    score[slot][:], q_stack[0:SPLIT, unit % NQ, j, t * P:(t + 1) * P],
                    k_stack[0:SPLIT, g * QUAD + j, h * HALF:(h + 1) * HALF], start=True, stop=True))
                dve.wait(scored, *released(f"maxes{unit % 2}"))
                maxed[unit] = dve.mark(lambda e, h=h, slot=slot: e.reduce_max(
                    maxes[:, unit % 2, h, t, j:j + 1], score[slot][:], AX.X))
                free[f"score{slot}"] = [maxed[unit]]

        def split_max(unit):
            u = unit % 2
            dve.wait(maxed[unit])
            whole = dve.mark(lambda e: e.tensor_tensor(max_row[:], maxes[:, u, 0], maxes[:, u, 1], ALU.max))
            free[f"maxes{u}"] = [whole]
            dve.wait(whole, *released(f"neg_max{u}"))
            high = dve.mark(lambda e: e.tensor_scalar(
                neg_max[:, u, :, 0:QUAD], max_row[:], -1.0, None, ALU.mult))
            dve.wait(high)
            return dve.mark(lambda e: e.scalar_tensor_tensor(
                out=neg_max[:, u, :, QUAD:2 * QUAD], in0=max_row[:], scalar=-1.0,
                in1=neg_max[:, u, :, 0:QUAD].bitcast(F32), op0=ALU.mult, op1=ALU.subtract))

        def place_max(unit, split):
            u, slot = unit % 2, n_score[0] % 3
            n_score[0] += 1
            pe.wait(split, ident_ready, *released(f"score{slot}"))
            for t in range(TPC):
                step = lambda e, t=t: e.matmul(
                    score[slot][SPLIT:ROWS, t * P:(t + 1) * P], neg_max[:, u, t, :].bitcast(F32), ident[:],
                    start=True, stop=True, tile_position=(0, SPLIT))
                pe.do(step) if t < TPC - 1 else None
            turned = pe.mark(step)
            free[f"neg_max{u}"] = [turned]
            act.wait(turned, *released(f"q_stack{unit % NQ}"))
            shift_ready[unit] = act.mark(lambda e: e.activation(
                q_stack[SPLIT:ROWS, unit % NQ, :, :],
                score[slot][SPLIT:ROWS, 0:CH].unsqueeze(1).to_broadcast([2 * QUAD, QUAD, CH]), ACT.Copy))
            free[f"score{slot}"] = [shift_ready[unit]]

        exped = {}
        paired = {}
        quads = {}
        p_free = {}

        def pass2(b, unit, kt, n):
            g = unit % G
            pe.wait(shift_ready[unit], hot_ready)
            for h in range(2):
                i = (2 * n + h) % 3
                pe.wait(*released(f"scoreT{i}"))
                for j in range(2 * h, 2 * h + 2):
                    step = lambda e, j=j: e.matmul(
                        scoreT[i][:, (j % 2) * CH:(j % 2 + 1) * CH],
                        k_stack[0:ROWS, g * QUAD + j, kt * P:(kt + 1) * P],
                        q_stack[0:ROWS, unit % NQ, j, :], start=True, stop=True)
                    pe.do(step) if j % 2 == 0 else None
                scored = pe.mark(step)
                act.wait(scored, *p_free.get(n - NP, released("early")))
                exped[n] = act.mark(lambda e: e.activation(
                    p_ring[:, n % NP, h * HALF:(h + 1) * HALF], scoreT[i][:], ACT.Exp, scale=SCALE))
                free[f"scoreT{i}"] = [exped[n]]
            scores2_done[unit] = scored
            free[f"q_stack{unit % NQ}"] = [scored]

        def add_pair(n):
            i = (n // 2) % 2
            pool.wait(exped[n], *released(f"pair{i}"), *released("early"))
            paired[n // 2] = pool.mark(lambda e: e.tensor_tensor(
                pair_sum[:, i, :], p_ring[:, (n - 1) % NP, :], p_ring[:, n % NP, :], ALU.add))

        def add_quad(n):
            dve.wait(paired[n // 2], *released("quad"), *released("early"))
            quads[n // 4] = dve.mark(lambda e: e.tensor_tensor(
                quad_sum[:], pair_sum[:, 0, :], pair_sum[:, 1, :], ALU.add))
            free["pair0"] = free["pair1"] = [quads[n // 4]]

        def value_product(b, unit, kt, n):
            pe.wait(exped[n], v_ready[b])
            if kt == 0:
                pe.wait(*released("acc"))
            for j in range(QUAD):
                head = (unit % G) * QUAD + j
                step = lambda e, j=j, head=head: e.matmul(
                    acc[j * DK:(j + 1) * DK, 0:CH], v_sb[:, kt, head * DK:(head + 1) * DK],
                    p_ring[:, n % NP, j * CH:(j + 1) * CH], start=kt == 0, stop=kt == KT - 1,
                    tile_position=(0, j * DK), skip_group_check=True)
                pe.do(step) if j < QUAD - 1 else None
            used = pe.mark(step)
            p_free[n] = [used, paired[n // 2]]
            return used

        def denominator(unit, n, first, last):
            pe.wait(quads[n // 4], ones_ready)
            for j in range(QUAD):
                step = lambda e, j=j: e.matmul(
                    acc[j * DK:(j + 1) * DK, CH:2 * CH], ones[:, 0:DK], quad_sum[:, j * CH:(j + 1) * CH],
                    start=False, stop=last, tile_position=(0, j * DK), skip_group_check=True)
                pe.do(step) if j < QUAD - 1 else None
            summed = pe.mark(step)
            free["quad"] = [summed]
            return summed

        out_done = {}

        def normalise(b, unit, summed):
            chunk, g = b * NC + unit // G % NC, unit % G
            i = chunk % 2
            dve.wait(summed, *released(f"outT{i}"))
            turned = dve.mark(lambda e: e.transpose(outT[:, i, g, :], acc[:, CH:2 * CH]))
            dve.wait(turned)
            inverse = dve.mark(lambda e: e.reciprocal(
                den_inverse[:], outT[:, i, g, :].rearrange("p (a b) -> p a b", b=DK)[:, :, 0]))
            dve.wait(inverse)
            back = dve.mark(lambda e: e.transpose(
                outT[:, i, g, :].rearrange("p (a b) -> p a b", b=DK),
                den_inverse[:].unsqueeze(2).to_broadcast([P, CH // DK, DK])))
            dve.wait(back)
            out_done[chunk] = dve.mark(lambda e: e.tensor_tensor(
                outT[:, i, g, :], acc[:, 0:CH], outT[:, i, g, :], ALU.mult))
            free["acc"] = [out_done[chunk]]

        def layer_norm(src, ready, gamma, beta, scratch, dst, dst_name):
            dve.wait(ready)
            counted = dve.mark(lambda e: e.bn_stats(stats[:], src))
            yield
            dve.wait(counted)
            aggregated = dve.mark(lambda e: e.bn_aggr(mean_var[:], stats[:]))
            dve.wait(aggregated)
            added = dve.mark(lambda e: e.tensor_scalar(var_eps[:], mean_var[:, 1:2], LN_EPS, None, ALU.add))
            pool.wait(added, half_ready)
            root = pool.mark(lambda e: e.tensor_tensor(rstd[:], var_eps[:], minus_half[:], ALU.pow))
            yield
            dve.wait(root)
            normal = dve.mark(lambda e: e.tensor_scalar(
                scratch, src, mean_var[:, 0:1], rstd[:], ALU.subtract, ALU.mult))
            pool.wait(normal)
            scaled = pool.mark(lambda e: e.tensor_tensor(scratch, scratch, rows_sb[gamma][:], ALU.mult))
            pool.wait(scaled, *released(dst_name))
            yield pool.mark(lambda e: e.tensor_tensor(dst, scratch, rows_sb[beta][:], ALU.add))

        n_nat = [0]

        def finish_chunk(chunk):
            b, k = divmod(chunk, NC)
            for t in range(TPC):
                token = k * CH + t * P
                i = n_nat[0] % 2
                n_nat[0] += 1
                sp.wait(*released(f"x_nat{i}"))
                land[f"x_nat{i}"].dma(sp, lambda e: e.dma_start(x_nat[:, i, :], x[b, token:token + P, :]))
                loaded = land[f"x_nat{i}"].mark()
                pool.wait(loaded, land_rows)
                biased = pool.mark(lambda e: e.tensor_tensor(
                    x_nat[:, i, :], x_nat[:, i, :], rows_sb["bo"][:], ALU.add))
                yield
                pe.wait(out_done[chunk], land["wo"].mark(), *released("misc"))
                for g in range(G):
                    step = lambda e, g=g: e.matmul(misc[:], outT[:, chunk % 2, g, t * P:(t + 1) * P],
                                                   wo[:, g, :], start=g == 0, stop=g == G - 1)
                    pe.do(step) if g < G - 1 else None
                projected = pe.mark(step)
                free[f"outT{chunk % 2}"] = [projected]
                dve.wait(projected, biased, *released("y"))
                y = dve.mark(lambda e: e.tensor_tensor(y_sb[:], misc[:], x_nat[:, i, :], ALU.add))
                free["misc"] = [y]
                free[f"x_nat{i}"] = [y]
                yield
                x1 = None
                for x1 in layer_norm(y_sb[:], y, "gamma0", "beta0", y_sb[:], x1_sb[:], "x1"):
                    yield
                free["y"] = [x1]
                yield
                for phi in elu(x1_sb[:], [x1], e_sb[:, 0, :], "e0", phi_sb[:], "phi"):
                    yield
                dve.wait(phi, *kv_ready[b])
                dotted = dve.mark(lambda e: e.tensor_tensor_reduce(
                    out=e_sb[:, 1, :], in0=phi_sb[:], in1=ksum_sb[:], scale=1.0, scalar=0.0,
                    op0=ALU.mult, op1=ALU.add, accum_out=z_sb[:, 0:1]))
                dve.wait(dotted)
                shifted = dve.mark(lambda e: e.tensor_scalar(z_sb[:, 1:2], z_sb[:, 0:1], ATTN_EPS, None, ALU.add))
                dve.wait(shifted)
                z = dve.mark(lambda e: e.reciprocal(z_sb[:, 2:3], z_sb[:, 1:2]))
                yield
                pe.wait(phi, ident_ready, *released("misc"))
                for d in range(G):
                    step = lambda e, d=d: e.matmul(
                        misc[:, d * P:(d + 1) * P], phi_sb[:, d * P:(d + 1) * P], ident[:],
                        start=True, stop=True, is_transpose=True)
                    pe.do(step) if d < G - 1 else None
                turned = pe.mark(step)
                free["phi"] = [turned, dotted]
                act.wait(turned, *released("phiT"))
                kept = act.mark(lambda e: e.activation(phiT_sb[:], misc[:], ACT.Copy))
                free["misc"] = [kept]
                yield
                pe.wait(kept, *kv_ready[b], *released("misc"))
                for d in range(G):
                    step = lambda e, d=d: e.matmul(misc[:], phiT_sb[:, d * P:(d + 1) * P], kv_sb[:, d, :],
                                                   start=d == 0, stop=d == G - 1)
                    pe.do(step) if d < G - 1 else None
                attended = pe.mark(step)
                free["phiT"] = [attended]
                free["kv"] = [attended, dotted]
                dve.wait(attended, z, x1, *released("y"))
                y = dve.mark(lambda e: e.scalar_tensor_tensor(
                    out=y_sb[:], in0=misc[:], scalar=z_sb[:, 2:3], in1=x1_sb[:], op0=ALU.mult, op1=ALU.add))
                free["misc"] = [y]
                free["x1"] = [y]
                yield
                for result in layer_norm(y_sb[:], y, "gamma1", "beta1", y_sb[:], x_nat[:, i, :], f"x_nat{i}"):
                    yield
                free["y"] = [result]
                sp.wait(result)
                land[f"out{i}"].dma(sp, lambda e: e.dma_start(out[b, token:token + P, :], x_nat[:, i, :]))
                free[f"x_nat{i}"] = [land[f"out{i}"].mark()]
                yield

        background = []

        def fill():
            while background:
                try:
                    next(background[0])
                    return
                except StopIteration:
                    background.pop(0)

        load_xT(0)
        load_xT(1)
        for unit in range(NQ):
            project_q(unit)
            stack_q(unit)
        for b in range(B):
            keys_and_values(b, fill)
            while background:
                fill()
            linear_sums(b)
            first = b * UNITS
            total = UNITS * STEPS
            splits = {}
            def pass1_step(m):
                if m < total:
                    pass1(b, first + m // STEPS, m % STEPS)
                    if m % STEPS == STEPS - 1:
                        splits[m // STEPS] = split_max(first + m // STEPS)
                if m % STEPS == 0 and 0 < m <= total:
                    place_max(first + m // STEPS - 1, splits[m // STEPS - 1])
            for m in range(STEPS + LEAD):
                pass1_step(m)
            last_value = None
            for n in range(total + LAG + 4):
                unit, kt = first + n // STEPS, n % STEPS
                if n < total:
                    pass2(b, unit, kt, n)
                q = n - 3
                if q % 4 == 3 and 0 <= q < total:
                    add_quad(q)
                q = n - 1
                if q % 2 and 0 < q < total:
                    add_pair(q)
                q = n - LAG
                if 0 <= q < total:
                    last_value = value_product(b, first + q // STEPS, q % STEPS, q)
                q = n - 5 
                if q % 4 == 3 and 0 <= q < total:
                    end = q % STEPS == STEPS - 1
                    summed = denominator(first + q // STEPS, q, q % STEPS == 3, end)
                    sums_done = summed
                q = n - LAG
                if q % STEPS == STEPS - 1 and 0 <= q < total:
                    normalise(b, q // STEPS, last_value)
                    if (q // STEPS) % G == G - 1:
                        background.append(finish_chunk(b * NC + q // STEPS // G))
                pass1_step(n + STEPS + LEAD)
                fresh = unit + NQ
                if n < total and fresh < B * UNITS:
                    if kt == 4:
                        project_q(fresh)
                    if kt == STEPS - 1:
                        stack_q(fresh)
                fill()
            free["k_stack"] = [scores2_done[first + UNITS - 1]]
            free["v_sb"] = [last_value]
            free["p_ring"] = [last_value, quads[total // 4 - 1], paired[total // 2 - 1], *free["quad"]]
            p_free.clear()
        while background:
            fill()
        sp.wait(land["out0"].mark(), land["out1"].mark())


def kernel(x, ctx_1024, L0_xattn_Wq, L0_xattn_bq, L0_xattn_Wk, L0_xattn_bk, L0_xattn_Wv, L0_xattn_bv,
           L0_xattn_Wo, L0_xattn_bo, L0_xattn_gamma, L0_xattn_beta, L1_xattn_gamma, L1_xattn_beta):
    import numpy as np
    import concourse.bacc as bacc
    from concourse.bass_utils import run_bass_kernel_spmd

    def turned(a):
        return np.ascontiguousarray(np.swapaxes(np.asarray(a), -1, -2))

    ins = {
        "x_in": x, "xT_in": turned(x), "ctx_in": ctx_1024, "ctxT_in": turned(ctx_1024),
        "WqT_in": turned(L0_xattn_Wq), "bq_in": L0_xattn_bq, "WkT_in": turned(L0_xattn_Wk), "bk_in": L0_xattn_bk,
        "WvT_in": turned(L0_xattn_Wv), "bv_in": L0_xattn_bv, "WoT_in": turned(L0_xattn_Wo), "bo_in": L0_xattn_bo,
        "gamma0_in": L0_xattn_gamma, "beta0_in": L0_xattn_beta,
        "gamma1_in": L1_xattn_gamma, "beta1_in": L1_xattn_beta,
    }
    nc = bacc.Bacc("TRN2", target_bir_lowering=False, num_devices=1)
    arrays = {n: np.ascontiguousarray(a) for n, a in ins.items()}
    aps = [nc.dram_tensor(n, a.shape, mybir.dt.from_np(a.dtype), kind="ExternalInput").ap() for n, a in arrays.items()]
    res = nc.dram_tensor("res_out", arrays["x_in"].shape, F32, kind="ExternalOutput").ap()
    build(nc, *aps, res)
    return run_bass_kernel_spmd(nc, [arrays], core_ids=[0]).results[0]["res_out"]
```

```python
from contextlib import ExitStack

import concourse.bass as bass
from concourse import mybir

F32 = mybir.dt.float32
F32R = mybir.dt.float32r
ALU = mybir.AluOpType
ACT = mybir.ActivationFunctionType
AX = mybir.AxisListType


class Stream:

    def __init__(self, engine, sem):
        self.engine, self.sem, self.count, self.seen = engine, sem, 0, {}

    def wait(self, *marks):
        for sem, value in marks:
            if self.seen.get(id(sem), 0) < value:
                self.seen[id(sem)] = value
                self.engine.wait_ge(sem, value)

    def do(self, instruction):
        instruction(self.engine)

    def mark(self, instruction):
        self.count += 1
        instruction(self.engine).then_inc(self.sem, 1)
        return self.sem, self.count


class Landing:

    def __init__(self, sem):
        self.sem, self.count = sem, 0

    def dma(self, stream, start):
        self.count += 16
        stream.do(lambda e: start(e).then_inc(self.sem, 16))

    def mark(self):
        return self.sem, self.count


def build(nc, x, xT, ctx, ctxT, WqT, bq, WkT, bk, WvT, bv, WoT, bo, gamma0, beta0, gamma1, beta1, out):
    B, S, D = x.shape
    P = nc.NUM_PARTITIONS
    DK = 32
    QUAD = P // DK
    G = D // P
    CH = 256
    NC = S // CH
    TPC = CH // P
    KT = S // P
    STEPS = KT
    HALF = 512
    SCALE = float(DK) ** -0.5
    LN_EPS, ATTN_EPS = 1e-5, 1e-6
    LEAD = 3
    LAG = 5
    NQ, NP, NSTAGE = 3, 7, 2
    SPLIT = 3 * DK
    ROWS = SPLIT + 2 * QUAD
    UNITS = NC * G

    with ExitStack() as c:
        def sb(name, shape, dt=F32):
            return c.enter_context(nc.sbuf_tensor(name, shape, dt))

        def ps(name, cols):
            return c.enter_context(nc.psum_tensor(name, [P, cols], F32))

        def sem(name):
            return c.enter_context(nc.semaphore(name))

        wq = sb("wq", [P, G, D])
        wo = sb("wo", [P, G, D])
        k_stack = sb("k_stack", [P, G * QUAD, S], F32R)
        q_stack = sb("q_stack", [P, NQ, QUAD, CH], F32R)
        v_sb = sb("v_sb", [P, KT, D])
        xT_sb = sb("xT_sb", [P, 2, G, CH])
        stage_h = sb("stage_h", [P, NSTAGE, CH], F32R)
        stage_l = sb("stage_l", [P, NSTAGE, CH], F32R)
        outT = sb("outT", [P, 2, G, CH])
        kv_sb = sb("kv_sb", [P, G, D])
        ksum_sb = sb("ksum_sb", [P, D])
        x_nat = sb("x_nat", [P, 2, D])
        y_sb = sb("y_sb", [P, TPC, D])
        e_sb = sb("e_sb", [P, 2, D])
        phi_sb = sb("phi_sb", [P, D])
        phiT_sb = sb("phiT_sb", [P, D])
        rows_sb = {n: sb(n + "_row", [P, D]) for n in ("bo", "gamma0", "beta0", "gamma1", "beta1")}
        bq_col = sb("bq_col", [P, G])
        bk_col = sb("bk_col", [P, G])
        bv_col = sb("bv_col", [P, G])
        ident = sb("ident", [P, P])
        ones = sb("ones", [P, P])
        onehot = sb("onehot", [P, QUAD])
        maxes = sb("maxes", [P, 2, 2, TPC, QUAD])
        max_row = sb("max_row", [P, TPC, QUAD])
        neg_max = sb("neg_max", [P, 2, TPC, 2 * QUAD], F32R)
        stats = sb("stats", [P, TPC, 6])
        mean_var = sb("mean_var", [P, TPC, 2])
        var_eps = sb("var_eps", [P, TPC, 1])
        neg_mean = sb("neg_mean", [P, TPC, 1])
        rstd = sb("rstd", [P, TPC, 1])
        shift = sb("shift", [P, TPC, 1])
        minus_half = sb("minus_half", [P, 1])
        z_sb = sb("z_sb", [P, TPC, 3])
        den_rows = sb("den_rows", [P, CH])
        den_inverse = sb("den_inverse", [P, CH // DK])
        with ExitStack() as early:
            def sb_early(name, shape, dt=F32):
                return early.enter_context(nc.sbuf_tensor(name, shape, dt))

            wv = sb_early("wv", [P, G, D])
            wk = sb_early("wk", [P, G, D])
            ctxT_sb = sb_early("ctxT_sb", [P, S // HALF, G, HALF])
            k_high = sb_early("k_high", [P, HALF], F32R)
            k_low = sb_early("k_low", [P, HALF], F32R)
        p_ring = sb("p_ring", [P, NP, QUAD * CH])
        pair_sum = sb("pair_sum", [P, 2, QUAD * CH])
        quad_sum = sb("quad_sum", [P, QUAD * CH])
        scoreT = [ps(f"scoreT{i}", HALF) for i in range(3)]
        score = [ps(f"score{i}", HALF) for i in range(3)]
        acc = ps("acc", HALF)
        misc = ps("misc", HALF)

        pe, act, dve, pool, sp = (Stream(engine, sem(name)) for engine, name in (
            (nc.tensor, "pe"), (nc.scalar, "act"), (nc.vector, "dve"), (nc.gpsimd, "pool"), (nc.sync, "sp")))
        land = {n: Landing(sem("dma_" + n)) for n in
                ("wq", "wo", "wk0", "wk1", "wk2", "wk3", "wv", "rows", "cols", "xT0", "xT1", "ctxT0", "ctxT1",
                 "x_nat0", "x_nat1", "out0", "out1", "last_out0", "last_out1")}
        free = {}

        def released(name):
            return free.get(name, [])

        PAUSE = 6
        EVAC = 3
        background = []
        features_ahead = []
        urgent = []
        prompt = []
        held = set()

        def acquire(name):
            while name in held:
                yield "blocked"
            held.add(name)

        def release(name):
            held.remove(name)

        def pause(pieces):
            for _ in range(pieces):
                yield

        def advance():
            for chain in list(prompt):
                if next(chain, "done") == "done":
                    prompt.remove(chain)

        def fill(pieces=1):
            for _ in range(pieces):
                for queue, work in ([(urgent, w) for w in urgent[:1]] + [(background, w) for w in background[:2]] +
                                    [(features_ahead, w) for w in features_ahead[:1] if not background]):
                    state = next(work, "done")
                    if state == "done":
                        queue.remove(work)
                    elif state == "blocked":
                        continue
                    elif queue is background:
                        background[0:2] = background[0:2][::-1]
                    break

        cleared = pool.mark(lambda e: e.memset(ident[:], 0.0))
        hot_cleared = pool.mark(lambda e: e.memset(onehot[:], 0.0))
        pool.wait(cleared)
        ident_ready = pool.mark(lambda e: e.affine_select(
            out=ident[:], in_=ident[:], compare_op=ALU.not_equal, fill=1.0, base=0,
            pattern=[[-1, P]], channel_multiplier=1))
        hot = hot_cleared
        for r in range(2):
            pool.wait(hot)
            hot = pool.mark(lambda e, r=r: e.affine_select(
                out=onehot[:], in_=onehot[:], compare_op=ALU.not_equal, fill=1.0,
                base=-(SPLIT + r * QUAD), pattern=[[-1, QUAD]], channel_multiplier=1))
        ones_ready = pool.mark(lambda e: e.memset(ones[:], 1.0))
        half_ready = pool.mark(lambda e: e.memset(minus_half[:], -0.5))
        dve.wait(hot)
        for g in range(G):
            hot_ready = dve.mark(lambda e, g=g: e.tensor_copy(
                k_stack[SPLIT:ROWS, g * QUAD:(g + 1) * QUAD, :],
                onehot[SPLIT:ROWS, :].unsqueeze(2).to_broadcast([2 * QUAD, QUAD, S])))

        for dst, src in ((bq_col, bq), (bk_col, bk), (bv_col, bv)):
            land["cols"].dma(sp, lambda e, d=dst, s=src: e.dma_start(
                d[:], s.rearrange("(t p) -> p t", p=P), allow_slow_non_contiguous=True))
        land_cols = land["cols"].mark()
        land_rows = (land["rows"].sem, 5 * 16)

        def load_rest():
            for name, src in (("bo", bo), ("gamma0", gamma0), ("beta0", beta0),
                              ("gamma1", gamma1), ("beta1", beta1)):
                land["rows"].dma(sp, lambda e, n=name, s=src: e.dma_start(
                    rows_sb[n][:], s.partition_broadcast(P)))
            land["wq"].dma(sp, lambda e: e.dma_start(wq[:], WqT.rearrange("(t p) n -> p t n", p=P)))
            land["wo"].dma(sp, lambda e: e.dma_start(wo[:], WoT.rearrange("(t p) n -> p t n", p=P)))
            load_xT(0)
            load_xT(1)

        n_stage = [0]
        stage_land = [Landing(sem(f"dma_stage{i}")) for i in range(NSTAGE)]
        k_stage_land = [(Landing(sem(f"dma_k_stage{i}")), Landing(sem(f"dma_k_stage{i}_pool"))) for i in range(2)]

        def project_split(weight, bias, src, g, bank, bank_name, high_out, low_out, landed):
            pe.wait(*released(bank_name))
            for t in range(G - 1):
                pe.do(lambda e: e.matmul(bank, weight[:, t, g * P:(g + 1) * P], src[:, t, :],
                                         start=t == 0, stop=False))
                if t % 2:
                    yield
            projected = pe.mark(lambda e: e.matmul(bank, weight[:, G - 1, g * P:(g + 1) * P], src[:, G - 1, :],
                                                   start=False, stop=True))
            yield
            act.wait(projected, land_cols, *landed)
            high = act.mark(lambda e: e.activation(high_out, bank, ACT.Identity, bias=bias[:, g:g + 1]))
            yield
            dve.wait(projected, high, *landed)
            low = dve.mark(lambda e: e.scalar_tensor_tensor(
                out=low_out, in0=bank, scalar=bias[:, g:g + 1], in1=high_out.bitcast(F32),
                op0=ALU.add, op1=ALU.subtract))
            free[bank_name] = [high, low]
            yield projected, high, low

        def stack(high_src, low_src, high, low, parts, dst, routes):
            for j in range(QUAD):
                for r, part in enumerate(parts):
                    src = high_src if part == "h" else low_src
                    queue, landing = routes[r]
                    queue.wait(high, low)
                    landing.dma(queue, lambda e: e.dma_start(
                        dst(j)[r * DK:(r + 1) * DK, :].bitcast(F32), src[j * DK:(j + 1) * DK, :].bitcast(F32)))
            return [landing.mark() for _, landing in routes]

        xT_ready, q_staged, q_ready = {}, {}, {}
        scores2_done = {}
        score1_done = {}

        def load_xT(chunk):
            b, k = divmod(chunk, NC)
            i = chunk % 2
            sp.wait(*released(f"xT{i}"))
            land[f"xT{i}"].dma(sp, lambda e: e.dma_start(
                xT_sb[:, i, :, :], xT[b, :, k * CH:(k + 1) * CH].rearrange("(t p) n -> p t n", p=P)))
            xT_ready[chunk] = land[f"xT{i}"].mark()

        def project_q(unit):
            chunk, g = divmod(unit, G)
            pe.wait(land["wq"].mark(), xT_ready[chunk])
            slot = n_stage[0] % NSTAGE
            n_stage[0] += 1
            yield from acquire("misc")
            for marks in project_split(
                wq, bq_col, xT_sb[:, chunk % 2, :, :], g, misc[:, 0:CH], "misc",
                stage_h[:, slot, :], stage_l[:, slot, :],
                    [used.mark() for used in (stage_land[slot], *k_stage_land[0])]):
                yield
            projected, high, low = marks
            yield from pause(EVAC)
            release("misc")
            q_staged[unit] = slot, high, low
            if g == G - 1:
                free[f"xT{chunk % 2}"] = [projected]
                if chunk + 2 < B * NC:
                    load_xT(chunk + 2)

        def stack_q(unit):
            slot, high, low = q_staged[unit]
            i = unit % NQ
            sp.wait(*released(f"q_stack{i}"))
            q_ready[unit] = stack(stage_h[:, slot, :], stage_l[:, slot, :], high, low, "hhl",
                                  lambda j: q_stack[:, i, j, :], [(sp, stage_land[slot])] * 3)

        k_ready, v_ready, kv_ready = {}, {}, {}
        spare = [("scoreT0", scoreT[0]), ("scoreT1", scoreT[1]), ("scoreT2", scoreT[2]), ("acc", acc)]

        def first_queries(unit):
            yield from project_q(unit)
            stack_q(unit)

        def fold_value_bias():
            dve.wait(land_cols)
            spread = dve.mark(lambda e: e.tensor_copy(
                y_sb[:, 0, :].rearrange("p (g n) -> p g n", g=G), bv_col[:].unsqueeze(2).to_broadcast([P, G, P])))
            pe.wait(spread, land["wo"].mark(), *released("misc"))
            for g in range(G):
                step = lambda e: e.matmul(misc[:], y_sb[:, 0, g * P:(g + 1) * P], wo[:, g, :],
                                          start=g == 0, stop=g == G - 1)
                pe.do(step) if g < G - 1 else None
            passed = pe.mark(step)
            free["y0"] = [passed]
            dve.wait(passed, land_rows)
            folded = dve.mark(lambda e: e.tensor_tensor(
                rows_sb["bo"][:], misc[:], rows_sb["bo"][:], ALU.add))
            free["misc"] = [folded]
            return folded

        early_loads = {}

        def load_wk(b):
            early_loads[b] = [], []
            for g in range(G):
                land[f"wk{g}"].dma(sp, lambda e: e.dma_start(
                    wk[:, :, g * P:(g + 1) * P],
                    WkT[:, g * P:(g + 1) * P].rearrange("(t p) n -> p t n", p=P)))
                early_loads[b][0].append(land[f"wk{g}"].mark())
                if g == 0 and b == 0:
                    load_ctxT(b, 0)
                    load_ctxT(b, 1)
                    load_wv()

        def load_ctxT(b, h):
            cols = slice(h * HALF, (h + 1) * HALF)
            land[f"ctxT{h}"].dma(sp, lambda e: e.dma_start(
                ctxT_sb[:, h, :, :], ctxT[b, :, cols].rearrange("(t p) n -> p t n", p=P)))
            early_loads[b][1].append(land[f"ctxT{h}"].mark())

        def load_wv():
            land["wv"].dma(sp, lambda e: e.dma_start(wv[:], WvT.rearrange("(t p) n -> p t n", p=P)))

        def keys_and_values(b, beside):
            wk_ready, loaded = early_loads[b]
            n = 0
            for g in range(G):
                for h in range(S // HALF):
                    name, bank = spare[n % len(spare)]
                    n += 1
                    if h == 0:
                        high_out, low_out = (s[:].rearrange("p a n -> p (a n)") for s in (stage_h, stage_l))
                        users = [*k_stage_land[0], *stage_land]
                    else:
                        high_out, low_out = k_high[:], k_low[:]
                        users = k_stage_land[1]
                    landed = [used.mark() for used in users] + (released("pair1") if h else [])
                    landing, pool_landing = k_stage_land[h]
                    pe.wait(wk_ready[g], loaded[h])
                    for marks in project_split(wk, bk_col, ctxT_sb[:, h, :, :], g,
                                               bank[:], name, high_out, low_out, landed):
                        fill(3)
                    _, high, low = marks
                    for queue in (sp, pool):
                        queue.wait(*released("k_stack"))
                    k_ready[b, g] = k_ready.get((b, g), []) + \
                        stack(high_out, low_out, high, low, "hlh",
                              lambda j: k_stack[:, g * QUAD + j, h * HALF:(h + 1) * HALF],
                              [(sp, landing), (sp, landing), (pool, pool_landing) if b == 0 else (sp, landing)])
                    beside(g)
                for t in range(g * KT // G, (g + 1) * KT // G):
                    name, bank = spare[n % len(spare)]
                    n += 1
                    pe.wait(land["wv"].mark(), *loaded, *released(name))
                    for f in range(G):
                        step = lambda e, f=f: e.matmul(bank[:], ctxT_sb[:, t * P // HALF, f, t * P % HALF:t * P % HALF + P],
                                                       wv[:, f, :], start=f == 0, stop=f == G - 1)
                        if f < G - 1:
                            pe.do(step)
                            fill(3)
                    projected = pe.mark(step)
                    dve.wait(projected, *released("v_sb"))
                    v_ready[b] = dve.mark(lambda e: e.tensor_copy(v_sb[:, t, :], bank[:]))
                    free[name] = [v_ready[b]]
                    beside(g)
                if b == 0 and g > 0:
                    for _ in first_queries(g - 1):
                        pass
            free["early"] = [projected, *(mark for g in range(G) for mark in k_ready[b, g])]

        def elu(src, src_ready, e_tile, e_name, dst, dst_name):
            act.wait(*src_ready, *released(e_name))
            below = act.mark(lambda e: e.activation(e_tile, src, ACT.Relu, scale=-1.0))
            yield
            act.wait(below)
            grown = act.mark(lambda e: e.activation(e_tile, e_tile, ACT.Exp, scale=-1.0))
            yield
            act.wait(grown)
            less = act.mark(lambda e: e.activation(e_tile, e_tile, ACT.Copy, bias=-1.0))
            yield from pause(4)
            dve.wait(less, *src_ready, *released(dst_name))
            done = dve.mark(lambda e: e.scalar_tensor_tensor(
                out=dst, in0=src, scalar=0.0, in1=e_tile, op0=ALU.max, op1=ALU.add))
            free[e_name] = [done]
            yield done

        featured = {}

        def features(b, t):
            i = t % 2
            act.wait(*released(f"x_nat{i}"))
            ctx_nat = x_nat[:, i, :]
            land[f"x_nat{i}"].dma(act, lambda e: e.dma_start(ctx_nat, ctx[b, t * P:(t + 1) * P, :]))
            loaded = land[f"x_nat{i}"].mark()
            yield
            name, dst = (("phi", phi_sb), ("phiT", phiT_sb))[i]
            yield from pause(5)
            for done in elu(ctx_nat, [loaded], e_sb[:, i, :], f"e{i}", dst[:], name):
                yield
            featured[b, t] = loaded, done

        def linear_sums(b, fill_pass1):
            banks = [scoreT[0], scoreT[1], scoreT[2], acc]
            for t in range(KT):
                i = t % 2
                name, phi = (("phi", phi_sb), ("phiT", phiT_sb))[i]
                pe.wait(*featured[b, t], ones_ready, *released("misc"),
                        *released("scoreT0"), *released("scoreT1"), *released("scoreT2"), *released("acc"))
                for d in range(G):
                    pe.do(lambda e, d=d: e.matmul(banks[d][:], phi[:, d * P:(d + 1) * P], x_nat[:, i, :],
                                                  start=t == 0, stop=t == KT - 1))
                summed = pe.mark(lambda e: e.matmul(misc[:], ones[:], phi[:],
                                                    start=t == 0, stop=t == KT - 1))
                free[name] = [summed]
                free[f"x_nat{i}"] = [summed]
                fill_pass1(t)
                if t + 2 < KT:
                    for _ in features(b, t + 2):
                        pass
            act.wait(summed, *released("kv"))
            dve.wait(summed, *free.pop("kv", []))
            kept = [act.mark(lambda e, d=d: e.activation(kv_sb[:, d, :], banks[d][:], ACT.Copy))
                    for d in range(G)]
            sums = dve.mark(lambda e: e.tensor_copy(ksum_sb[:], misc[:]))
            for name, mark in zip(("scoreT0", "scoreT1", "scoreT2", "acc", "misc"), (*kept, sums)):
                free[name] = [mark]
            kv_ready[b] = [kept[3], sums]
            return summed

        n_score = [0]
        shift_ready = {}
        maxed = {}

        def pass1(b, unit, i, h):
            j, t = divmod(i, TPC)
            g = unit % G
            slot = n_score[0] % 3
            n_score[0] += 1
            pe.wait(*q_ready[unit], *k_ready[b, g], *released(f"score{slot}"))
            scored = pe.mark(lambda e: e.matmul(
                score[slot][:], q_stack[0:SPLIT, unit % NQ, j, t * P:(t + 1) * P],
                k_stack[0:SPLIT, g * QUAD + j, h * HALF:(h + 1) * HALF], start=True, stop=True))
            dve.wait(scored, *released(f"maxes{unit % 2}"))
            maxed[unit] = dve.mark(lambda e: e.reduce_max(
                maxes[:, unit % 2, h, t, j:j + 1], score[slot][:], AX.X))
            free[f"score{slot}"] = [maxed[unit]]

        splits = {}

        def split_max(unit):
            u = unit % 2
            dve.wait(maxed[unit])
            whole = dve.mark(lambda e: e.tensor_tensor(max_row[:], maxes[:, u, 0], maxes[:, u, 1], ALU.max))
            free[f"maxes{u}"] = [whole]
            yield
            dve.wait(whole, *released(f"neg_max{u}"))
            high = dve.mark(lambda e: e.tensor_scalar(
                neg_max[:, u, :, 0:QUAD], max_row[:], -1.0, None, ALU.mult))
            yield
            dve.wait(high)
            splits[unit] = dve.mark(lambda e: e.scalar_tensor_tensor(
                out=neg_max[:, u, :, QUAD:2 * QUAD], in0=max_row[:], scalar=-1.0,
                in1=neg_max[:, u, :, 0:QUAD].bitcast(F32), op0=ALU.mult, op1=ALU.subtract))
            yield

        def place_max(unit):
            u, slot = unit % 2, n_score[0] % 3
            n_score[0] += 1
            pe.wait(splits[unit], ident_ready, *released(f"score{slot}"))
            for t in range(TPC):
                step = lambda e, t=t: e.matmul(
                    score[slot][SPLIT:ROWS, t * P:(t + 1) * P], neg_max[:, u, t, :].bitcast(F32), ident[:],
                    start=True, stop=True, tile_position=(0, SPLIT))
                pe.do(step) if t < TPC - 1 else None
            turned = pe.mark(step)
            free[f"neg_max{u}"] = [turned]
            act.wait(turned, *released(f"q_stack{unit % NQ}"))
            shift_ready[unit] = act.mark(lambda e: e.activation(
                q_stack[SPLIT:ROWS, unit % NQ, :, :],
                score[slot][SPLIT:ROWS, 0:CH].unsqueeze(1).to_broadcast([2 * QUAD, QUAD, CH]), ACT.Copy))
            free[f"score{slot}"] = [shift_ready[unit]]

        exped = {}
        paired = {}
        quads = {}
        p_free = {}

        def pass2(b, unit, kt, n, h):
            g = unit % G
            i = (2 * n + h) % 3
            pe.wait(shift_ready[unit], hot_ready, *released(f"scoreT{i}"))
            for j in range(2 * h, 2 * h + 2):
                step = lambda e: e.matmul(
                    scoreT[i][:, (j % 2) * CH:(j % 2 + 1) * CH],
                    k_stack[0:ROWS, g * QUAD + j, kt * P:(kt + 1) * P],
                    q_stack[0:ROWS, unit % NQ, j, :], start=True, stop=True)
                pe.do(step) if j % 2 == 0 else None
            scored = pe.mark(step)
            act.wait(scored, *p_free.get(n - NP, released("early")))
            exped[n] = act.mark(lambda e: e.activation(
                p_ring[:, n % NP, h * HALF:(h + 1) * HALF], scoreT[i][:], ACT.Exp, scale=SCALE))
            free[f"scoreT{i}"] = [exped[n]]
            scores2_done[unit] = scored
            free[f"q_stack{unit % NQ}"] = [scored]

        def add_pair(n, h):
            i = (n // 2) % 2
            cols = slice(h * HALF, (h + 1) * HALF)
            pool.wait(exped[n], *released(f"pair{i}"), *released("early"))
            paired[n // 2] = pool.mark(lambda e: e.tensor_tensor(
                pair_sum[:, i, cols], p_ring[:, (n - 1) % NP, cols], p_ring[:, n % NP, cols], ALU.add))

        def add_quad(n, h):
            cols = slice(h * HALF, (h + 1) * HALF)
            dve.wait(paired[n // 2], *released("quad"), *released("early"))
            quads[n // 4] = dve.mark(lambda e: e.tensor_tensor(
                quad_sum[:, cols], pair_sum[:, 0, cols], pair_sum[:, 1, cols], ALU.add))
            free["pair0"] = free["pair1"] = [quads[n // 4]]

        def value_product(b, unit, kt, n):
            pe.wait(exped[n], v_ready[b])
            if kt == 0:
                pe.wait(*released("acc"))
            for j in range(QUAD):
                head = (unit % G) * QUAD + j
                step = lambda e, j=j, head=head: e.matmul(
                    acc[j * DK:(j + 1) * DK, 0:CH], v_sb[:, kt, head * DK:(head + 1) * DK],
                    p_ring[:, n % NP, j * CH:(j + 1) * CH], start=kt == 0, stop=kt == KT - 1,
                    tile_position=(0, j * DK), skip_group_check=True)
                pe.do(step) if j < QUAD - 1 else None
            used = pe.mark(step)
            p_free[n] = [used, paired[n // 2]]
            return used

        def denominator(unit, n, last):
            pe.wait(quads[n // 4], ones_ready)
            for j in range(QUAD):
                step = lambda e, j=j: e.matmul(
                    acc[j * DK:(j + 1) * DK, CH:2 * CH], ones[:, 0:DK], quad_sum[:, j * CH:(j + 1) * CH],
                    start=False, stop=last, tile_position=(0, j * DK), skip_group_check=True)
                pe.do(step) if j < QUAD - 1 else None
            summed = pe.mark(step)
            free["quad"] = [summed]
            return summed

        out_done = {}

        def normalise(b, unit, value_sum, divisors):
            chunk, g = b * NC + unit // G % NC, unit % G
            i = chunk % 2
            dve.wait(divisors, *released("den_rows"))
            turned = dve.mark(lambda e: e.transpose(den_rows[:], acc[:, CH:2 * CH]))
            yield
            act.wait(turned, value_sum, *free.pop(f"outT{i}", []) if g == 0 else [])
            kept = act.mark(lambda e: e.activation(outT[:, i, g, :], acc[:, 0:CH], ACT.Copy))
            free["acc"] = [kept]
            yield
            dve.wait(turned)
            inverse = dve.mark(lambda e: e.reciprocal(
                den_inverse[:], den_rows[:].rearrange("p (a b) -> p a b", b=DK)[:, :, 0]))
            yield
            dve.wait(inverse)
            back = dve.mark(lambda e: e.transpose(
                den_rows[:].rearrange("p (a b) -> p a b", b=DK),
                den_inverse[:].unsqueeze(2).to_broadcast([P, CH // DK, DK])))
            yield
            dve.wait(back, kept)
            out_done[chunk] = dve.mark(lambda e: e.tensor_tensor(
                outT[:, i, g, :], outT[:, i, g, :], den_rows[:], ALU.mult))
            free["den_rows"] = [out_done[chunk]]
            if g == G - 1:
                background.extend(finish_tile(chunk, t) for t in range(TPC))
            yield

        def layer_norm(t, ready, gamma, beta, dst, dst_name):
            y, mv, eps_var, negative, root, offset = (
                buffer[:, t, :] for buffer in (y_sb, mean_var, var_eps, neg_mean, rstd, shift))
            dve.wait(ready)
            counted = dve.mark(lambda e: e.bn_stats(stats[:, t, :], y))
            dve.wait(counted)
            aggregated = dve.mark(lambda e: e.bn_aggr(mv, stats[:, t, :]))
            dve.wait(aggregated)
            dve.do(lambda e: e.tensor_scalar(negative, mv[:, 0:1], -1.0, None, ALU.mult))
            added = dve.mark(lambda e: e.tensor_scalar(eps_var, mv[:, 1:2], LN_EPS, None, ALU.add))
            yield
            pool.wait(added, half_ready)
            rooted = pool.mark(lambda e: e.tensor_tensor(root, eps_var, minus_half[:], ALU.pow))
            pool.wait(rooted)
            shifted = pool.mark(lambda e: e.tensor_tensor(offset, negative, root, ALU.mult))
            yield from pause(PAUSE)
            act.wait(shifted)
            normal = act.mark(lambda e: e.activation(y, y, ACT.Identity, scale=root, bias=offset))
            yield from pause(1)
            pool.wait(normal)
            scaled = pool.mark(lambda e: e.tensor_tensor(y, y, rows_sb[gamma][:], ALU.mult))
            yield
            pool.wait(scaled, *released(dst_name))
            yield pool.mark(lambda e: e.tensor_tensor(dst, y, rows_sb[beta][:], ALU.add))

        bias_folded = []

        def finish_tile(chunk, t):
            b, k = divmod(chunk, NC)
            token = k * CH + t * P
            y, z = y_sb[:, t, :], z_sb[:, t, :]
            yield from acquire(f"tile{t}")
            sp.wait(*released(f"x_nat{t}"))
            land[f"x_nat{t}"].dma(sp, lambda e: e.dma_start(x_nat[:, t, :], x[b, token:token + P, :]))
            loaded = land[f"x_nat{t}"].mark()
            yield from pause(PAUSE)
            yield from acquire("misc")
            pe.wait(out_done[chunk], land["wo"].mark(), *released("misc"))
            for g in range(G):
                step = lambda e: e.matmul(misc[:], outT[:, chunk % 2, g, t * P:(t + 1) * P],
                                          wo[:, g, :], start=g == 0, stop=g == G - 1)
                if g < G - 1:
                    pe.do(step)
                    yield
                if g == 1:
                    pool.wait(loaded, bias_folded[0])
                    biased = pool.mark(lambda e: e.tensor_tensor(
                        x_nat[:, t, :], x_nat[:, t, :], rows_sb["bo"][:], ALU.add))
            projected = pe.mark(step)
            free.setdefault(f"outT{chunk % 2}", []).append(projected)
            yield from pause(2)
            dve.wait(projected, biased, *released(f"y{t}"))
            summed = dve.mark(lambda e: e.tensor_tensor(y, misc[:], x_nat[:, t, :], ALU.add))
            free["misc"] = [summed]
            free[f"x_nat{t}"] = [summed]
            yield from pause(EVAC)
            release("misc")
            yield
            for x1 in layer_norm(t, summed, "gamma0", "beta0", y, f"y{t}"):
                yield
            yield from pause(PAUSE)
            yield from acquire("phi")
            for phi in elu(y, [x1], e_sb[:, t, :], f"e{t}", phi_sb[:], "phi"):
                yield
            dve.wait(phi, *kv_ready[b])
            dotted = dve.mark(lambda e: e.tensor_tensor_reduce(
                out=e_sb[:, t, :], in0=phi_sb[:], in1=ksum_sb[:], scale=1.0, scalar=0.0,
                op0=ALU.mult, op1=ALU.add, accum_out=z[:, 0:1]))
            yield
            dve.wait(dotted)
            added = dve.mark(lambda e: e.tensor_scalar(z[:, 1:2], z[:, 0:1], ATTN_EPS, None, ALU.add))
            yield
            dve.wait(added)
            inverted = dve.mark(lambda e: e.reciprocal(z[:, 2:3], z[:, 1:2]))
            yield from acquire("phiT")
            yield from acquire("misc")
            pe.wait(phi, ident_ready, *released("misc"))
            for d in range(G):
                step = lambda e, d=d: e.matmul(
                    misc[:, d * P:(d + 1) * P], phi_sb[:, d * P:(d + 1) * P], ident[:],
                    start=True, stop=True, is_transpose=True)
                pe.do(step) if d < G - 1 else None
            turned = pe.mark(step)
            free["phi"] = [turned, dotted]
            release("phi")
            yield
            act.wait(turned, *released("phiT"))
            kept = act.mark(lambda e: e.activation(phiT_sb[:], misc[:], ACT.Copy))
            free["misc"] = [kept]
            yield from pause(EVAC)
            release("misc")
            yield
            yield from acquire("misc")
            pe.wait(kept, *kv_ready[b], *released("misc"))
            for d in range(G):
                step = lambda e: e.matmul(misc[:], phiT_sb[:, d * P:(d + 1) * P], kv_sb[:, d, :],
                                          start=d == 0, stop=d == G - 1)
                if d < G - 1:
                    pe.do(step)
                    yield
            attended = pe.mark(step)
            free["phiT"] = [attended]
            release("phiT")
            free.setdefault("kv", []).extend([attended, dotted])
            yield
            dve.wait(attended, inverted, x1)
            summed = dve.mark(lambda e: e.scalar_tensor_tensor(
                out=y, in0=misc[:], scalar=z[:, 2:3], in1=y, op0=ALU.mult, op1=ALU.add))
            free["misc"] = [summed]
            yield from pause(EVAC)
            release("misc")
            yield
            for result in layer_norm(t, summed, "gamma1", "beta1", x_nat[:, t, :], f"x_nat{t}"):
                yield
            free[f"y{t}"] = [result]
            queue, landing = (pool, land[f"last_out{t}"]) if k == NC - 1 else (sp, land[f"out{t}"])
            if queue is sp:
                yield from pause(PAUSE)
            queue.wait(result)
            landing.dma(queue, lambda e: e.dma_start(out[b, token:token + P, :], x_nat[:, t, :]))
            free[f"x_nat{t}"] = [landing.mark()]
            release(f"tile{t}")
            yield

        for b in range(B):
            if b == 0:
                load_wk(b)
                load_rest()
            features_ahead.extend(features(b, t) for t in range(2))
            first = b * UNITS
            total = UNITS * STEPS

            def pass1_half(m, h):
                unit = m // STEPS
                if m % STEPS == 1 and h == 1 and 1 < m <= total + 1:
                    place_max(first + unit - 1)
                if m < total:
                    pass1(b, first + unit, m % STEPS, h)
                    if m % STEPS == STEPS - 1 and h == 1:
                        prompt.append(split_max(first + unit))
                advance()

            ahead = list(range(2 * (STEPS + LEAD)))

            def pass1_ahead(t):
                for _ in range(3 if t < KT - 1 else len(ahead)):
                    if ahead:
                        pass1_half(*divmod(ahead.pop(0), 2))

            def beside_keys(g):
                fill(3)
                if b > 0 and g > 0:
                    pass1_half(*divmod(ahead.pop(0), 2))

            keys_and_values(b, beside_keys)
            if b == 0:
                bias_folded.append(fold_value_bias())
            while background or urgent or features_ahead:
                fill()
            linear_sums(b, pass1_ahead)
            last_value = None
            for n in range(total + LAG + 2):
                unit, kt = first + n // STEPS, n % STEPS
                quad, pair = n - 3, n - 1
                add_quads = quad % 4 == 3 and 0 <= quad < total
                add_pairs = pair % 2 and 0 < pair < total
                pass1_half(n + STEPS + LEAD, 0)
                fill()
                if n < total:
                    pass2(b, unit, kt, n, 0)
                fill()
                for value in {0: [], 1: [n - LAG - 1, n - LAG]}.get((n - LAG) % STEPS, [n - LAG]):
                    if 0 <= value < total:
                        last_value = value_product(b, first + value // STEPS, value % STEPS, value)
                fill()
                pass1_half(n + STEPS + LEAD, 1)
                fill()
                if n < total:
                    pass2(b, unit, kt, n, 1)
                if add_quads:
                    add_quad(quad, 0)
                if add_pairs:
                    add_pair(pair, 0)
                fill()
                summed = n - LAG
                if summed % 4 == 3 and 0 <= summed < total:
                    divisors = denominator(first + summed // STEPS, summed, summed % STEPS == STEPS - 1)
                    if summed % STEPS == STEPS - 1:
                        prompt.append(normalise(b, summed // STEPS, last_value, divisors))
                if add_quads:
                    add_quad(quad, 1)
                if add_pairs:
                    add_pair(pair, 1)
                fresh = unit + NQ
                if n < total and fresh < B * UNITS:
                    if kt == 2:
                        urgent.append(project_q(fresh))
                    if kt == STEPS - 1:
                        while urgent:
                            fill()
                        if n < total - 1:
                            stack_q(fresh)
                if b + 1 < B and n == total:
                    sp.wait(*p_free[n - NP + 1], *p_free[n - NP + 2])
                    load_wk(b + 1)
                if b + 1 < B and n == total + 2:
                    sp.wait(*p_free[n - NP + 1], *p_free[n - NP + 2])
                    load_ctxT(b + 1, 0)
            while prompt:
                advance()
            free["k_stack"] = [scores2_done[first + UNITS - 1]]
            free["v_sb"] = [last_value]
            if b + 1 < B:
                sp.wait(*p_free[total - 2], *p_free[total - 1])
                load_wv()
                sp.wait(*released("pair0"))
                load_ctxT(b + 1, 1)
                stack_q(first + UNITS + NQ - 1)
            p_free.clear()
        while background:
            fill()
        sp.wait(*(land[name].mark() for name in ("out0", "out1", "last_out0", "last_out1")))


def kernel(x, ctx_1024, L0_xattn_Wq, L0_xattn_bq, L0_xattn_Wk, L0_xattn_bk, L0_xattn_Wv, L0_xattn_bv,
           L0_xattn_Wo, L0_xattn_bo, L0_xattn_gamma, L0_xattn_beta, L1_xattn_gamma, L1_xattn_beta):
    import numpy as np
    import concourse.bacc as bacc
    from concourse.bass_utils import run_bass_kernel_spmd

    def turned(a):
        return np.ascontiguousarray(np.swapaxes(np.asarray(a), -1, -2))

    ins = {
        "x_in": x, "xT_in": turned(x), "ctx_in": ctx_1024, "ctxT_in": turned(ctx_1024),
        "WqT_in": turned(L0_xattn_Wq), "bq_in": L0_xattn_bq, "WkT_in": turned(L0_xattn_Wk), "bk_in": L0_xattn_bk,
        "WvT_in": turned(L0_xattn_Wv), "bv_in": L0_xattn_bv, "WoT_in": turned(L0_xattn_Wo), "bo_in": L0_xattn_bo,
        "gamma0_in": L0_xattn_gamma, "beta0_in": L0_xattn_beta,
        "gamma1_in": L1_xattn_gamma, "beta1_in": L1_xattn_beta,
    }
    nc = bacc.Bacc("TRN2", target_bir_lowering=False, num_devices=1)
    arrays = {n: np.ascontiguousarray(a) for n, a in ins.items()}
    aps = [nc.dram_tensor(n, a.shape, mybir.dt.from_np(a.dtype), kind="ExternalInput").ap() for n, a in arrays.items()]
    res = nc.dram_tensor("res_out", arrays["x_in"].shape, F32, kind="ExternalOutput").ap()
    build(nc, *aps, res)
    return run_bass_kernel_spmd(nc, [arrays], core_ids=[0]).results[0]["res_out"]
```
